# Optimizing a Trainium2 kernel written in Bass

```python
import numpy as np
import jax
import jax.numpy as jnp

def _softmax(x, axis=-1):
    return jax.nn.softmax(x, axis=axis)

def _gelu(x):
    return jax.nn.gelu(x, approximate=True)

def _silu(x):
    return jax.nn.silu(x)

def _sigmoid(x):
    return jax.nn.sigmoid(x)

def _layernorm(x, axis=-1, eps=1e-05):
    m = jnp.mean(x, axis=axis, keepdims=True)
    v = jnp.var(x, axis=axis, keepdims=True)
    return (x - m) / jnp.sqrt(v + eps)

def _scatter_add(tgt, idx, src, axis=0):
    return tgt.at[idx].add(src)

def _segment_sum(src, seg, n):
    return jax.ops.segment_sum(src, seg, n)
kernel_name = 'mk_vit_tower_d1_tok_img768_r4_52bf28'

def setup_inputs(seed: int=0):
    np.random.seed(seed)
    _w = jnp.asarray

    def _rec_inputs():
        import jax
        import jax.numpy as jnp
        _rk = jax.random.key(seed)
        x = -0.000147625 + 0.999875 * jax.random.normal(jax.random.fold_in(_rk, 1), (64, 12, 224, 224), jnp.float32)
        return x
    x = _rec_inputs()

    def _L0_tok_setup():
        import jax, jax.numpy as jnp
        import numpy as np
        IMG = 224
        PATCH = 16
        EMBED = 192
        C = 12
        B = 64
        key = jax.random.key(seed)
        k1, k2 = jax.random.split(key)
        x = jax.random.normal(k1, (B, C, IMG, IMG), dtype=jnp.float32)
        channel_weights = jax.random.normal(k2, (C, EMBED), dtype=jnp.float32)
        return {'x': x, 'channel_weights': channel_weights}
    _L0_tok_all = _L0_tok_setup()
    _L0_tok_in = {k: v for k, v in _L0_tok_all.items() if k in ('channel_weights',)}
    del _L0_tok_all

    def _L0_attn_setup():
        import math
        import jax, jax.numpy as jnp
        import numpy as np
        NUM_HEADS = 12
        EPS = 0.0001

        def softmax_kernel_features(data, proj, is_query):
            d = data.shape[-1]
            data_normalizer = 1.0 / math.sqrt(math.sqrt(d))
            ratio = 1.0 / math.sqrt(proj.shape[0])
            data_dash = jnp.einsum('bhnd,md->bhnm', data_normalizer * data, proj)
            diag_data = jnp.sum(jnp.square(data), axis=-1, keepdims=True) * 0.5 * data_normalizer * data_normalizer
            if is_query:
                stab = jnp.max(data_dash, axis=-1, keepdims=True)
            else:
                stab = jnp.max(data_dash)
            return ratio * (jnp.exp(data_dash - diag_data - stab) + EPS)
        key = jax.random.key(seed)
        k0, k1, k2, k3, k4 = jax.random.split(key, 5)
        B, N, C, H = (8, 1024, 192, NUM_HEADS)
        hd = C // H
        m = int(hd * math.log(hd))
        x = jax.random.normal(k0, (B, N, C), dtype=jnp.float32)
        W_qkv = jax.random.normal(k1, (C, 3 * C), dtype=jnp.float32) / math.sqrt(C)
        W_proj = jax.random.normal(k2, (C, C), dtype=jnp.float32) / math.sqrt(C)
        b_proj = jnp.zeros((C,), dtype=jnp.float32)
        proj_mat = jax.random.normal(k3, (m, hd), dtype=jnp.float32)
        return {'x': x, 'W_qkv': W_qkv, 'W_proj': W_proj, 'b_proj': b_proj, 'proj_mat': proj_mat}
    _L0_attn_all = _L0_attn_setup()
    _L0_attn_in = {k: v for k, v in _L0_attn_all.items() if k in ('W_qkv', 'W_proj', 'b_proj', 'proj_mat')}
    del _L0_attn_all

    def _L0_ffn_setup():
        import jax, jax.numpy as jnp
        import numpy as np
        B, S, D, H, E, K = (1, 512, 192, 384, 8, 2)
        key = jax.random.key(seed)
        ks = jax.random.split(key, 6)
        scale_d = 1.0 / np.sqrt(D)
        scale_h = 1.0 / np.sqrt(H)
        return {'x': jax.random.normal(ks[0], (B, S, D), dtype=jnp.float32), 'Wg': jax.random.uniform(ks[1], (D, E), minval=-scale_d, maxval=scale_d, dtype=jnp.float32), 'W1': jax.random.uniform(ks[2], (E, D, H), minval=-scale_d, maxval=scale_d, dtype=jnp.float32), 'b1': jax.random.uniform(ks[3], (E, H), minval=-scale_d, maxval=scale_d, dtype=jnp.float32), 'W2': jax.random.uniform(ks[4], (E, H, D), minval=-scale_h, maxval=scale_h, dtype=jnp.float32), 'b2': jax.random.uniform(ks[5], (E, D), minval=-scale_h, maxval=scale_h, dtype=jnp.float32)}
    _L0_ffn_all = _L0_ffn_setup()
    _L0_ffn_in = {k: v for k, v in _L0_ffn_all.items() if k in ('Wg', 'W1', 'b1', 'W2', 'b2')}
    del _L0_ffn_all
    return {'x': x, 'L0_tok_channel_weights': _L0_tok_in['channel_weights'], 'L0_attn_W_qkv': _L0_attn_in['W_qkv'], 'L0_attn_W_proj': _L0_attn_in['W_proj'], 'L0_attn_b_proj': _L0_attn_in['b_proj'], 'L0_attn_proj_mat': _L0_attn_in['proj_mat'], 'L0_ffn_Wg': _L0_ffn_in['Wg'], 'L0_ffn_W1': _L0_ffn_in['W1'], 'L0_ffn_b1': _L0_ffn_in['b1'], 'L0_ffn_W2': _L0_ffn_in['W2'], 'L0_ffn_b2': _L0_ffn_in['b2']}

def reference(x, L0_tok_channel_weights, L0_attn_W_qkv, L0_attn_W_proj, L0_attn_b_proj, L0_attn_proj_mat, L0_ffn_Wg, L0_ffn_W1, L0_ffn_b1, L0_ffn_W2, L0_ffn_b2):
    import jax
    import jax.numpy as jnp

    def _L0_tok_ref(x, channel_weights):
        import jax, jax.numpy as jnp
        import numpy as np
        IMG = 224
        PATCH = 16
        EMBED = 192
        C = 12
        B = 64
        Bb, Cc, H, W = x.shape
        K = PATCH
        n = H // K
        pooled = x.reshape(Bb, Cc, n, K, n, K).sum(axis=(3, 5))
        out = jnp.einsum('bcij,ce->bije', pooled, channel_weights)
        return out.reshape(Bb, n * n, EMBED)

    def _L0_attn_ref(x, W_qkv, W_proj, b_proj, proj_mat):
        import math
        import jax, jax.numpy as jnp
        import numpy as np
        NUM_HEADS = 12
        EPS = 0.0001

        def softmax_kernel_features(data, proj, is_query):
            d = data.shape[-1]
            data_normalizer = 1.0 / math.sqrt(math.sqrt(d))
            ratio = 1.0 / math.sqrt(proj.shape[0])
            data_dash = jnp.einsum('bhnd,md->bhnm', data_normalizer * data, proj)
            diag_data = jnp.sum(jnp.square(data), axis=-1, keepdims=True) * 0.5 * data_normalizer * data_normalizer
            if is_query:
                stab = jnp.max(data_dash, axis=-1, keepdims=True)
            else:
                stab = jnp.max(data_dash)
            return ratio * (jnp.exp(data_dash - diag_data - stab) + EPS)
        B, N, C = x.shape
        H = NUM_HEADS
        hd = C // H
        qkv = (x @ W_qkv).reshape(B, N, 3, H, hd)
        qkv = jnp.transpose(qkv, (2, 0, 3, 1, 4))
        q, k, v = (qkv[0], qkv[1], qkv[2])
        q1 = softmax_kernel_features(q, proj_mat, is_query=True)
        k1 = softmax_kernel_features(k, proj_mat, is_query=False)
        kv = jnp.einsum('bhnm,bhnd->bhmd', k1, v)
        ksum = jnp.sum(k1, axis=2)
        z = 1.0 / jnp.einsum('bhnm,bhm->bhn', q1, ksum)
        out = jnp.einsum('bhnm,bhmd->bhnd', q1, kv) * z[..., None]
        out = jnp.transpose(out, (0, 2, 1, 3)).reshape(B, N, C)
        return out @ W_proj + b_proj

    def _L0_ffn_ref(x, Wg, W1, b1, W2, b2):
        import jax, jax.numpy as jnp
        import numpy as np
        B, S, D, H, E, K = (1, 512, 192, 384, 8, 2)
        gate_scores = jnp.einsum('bsd,de->bse', x, Wg)
        topk_scores, topk_idx = jax.lax.top_k(gate_scores, K)
        topk_probs = jax.nn.softmax(topk_scores, axis=-1)
        h = jax.nn.gelu(jnp.einsum('bsd,edh->bseh', x, W1) + b1, approximate=False)
        y = jnp.einsum('bseh,eho->bseo', h, W2) + b2
        y_sel = jnp.take_along_axis(y, topk_idx[..., None], axis=2)
        return jnp.sum(topk_probs[..., None] * y_sel, axis=2)
    h = _L0_tok_ref(x, L0_tok_channel_weights)
    h = h + _L0_attn_ref(_layernorm(h, axis=-1), L0_attn_W_qkv, L0_attn_W_proj, L0_attn_b_proj, L0_attn_proj_mat)
    h = h + _L0_ffn_ref(_layernorm(h, axis=-1), L0_ffn_Wg, L0_ffn_W1, L0_ffn_b1, L0_ffn_W2, L0_ffn_b2)
    return h

_drawn_inputs = setup_inputs


def setup_inputs(seed=0):
    import zlib

    import numpy as np

    out = dict(_drawn_inputs(seed))
    spreads = {'L0_attn_b_proj': (0.0, 2.0)}
    factors = {'L0_attn_W_qkv': 8.0,
     'L0_attn_W_proj': 8.0,
     'L0_attn_proj_mat': 64.0,
     'L0_ffn_Wg': 8.0,
     'L0_ffn_W1': 8.0,
     'L0_ffn_b1': 27.965,
     'L0_ffn_W2': 8.0,
     'L0_ffn_b2': 64.0}
    for name, (base, spread) in spreads.items():
        noise = np.random.default_rng([zlib.crc32(name.encode()), seed]).standard_normal(out[name].shape)
        drawn = base * np.exp(spread * noise) if base else spread * noise
        out[name] = jnp.asarray(drawn.astype(out[name].dtype))
    for name, factor in factors.items():
        out[name] = (out[name] * factor).astype(out[name].dtype)
    return out
```

```python
from contextlib import ExitStack

import concourse.bass as bass
from concourse import mybir

ALU = mybir.AluOpType
ACT = mybir.ActivationFunctionType
AX = mybir.AxisListType
F32 = mybir.dt.float32
BF16 = mybir.dt.bfloat16
I32 = mybir.dt.int32
U32 = mybir.dt.uint32

B, C, IMG, PATCH = 64, 12, 224, 16
NP = IMG // PATCH
TOK = NP * NP
HT = TOK // 2
NT = 2 * B
T = B * TOK
D = 192
NH, HD, M = 12, 16, 44
HM = NH * M
HALF = HM // 2
PAIRS = NH // 2
PM = 2 * M
UC = C + 1
UW = 32
WIN = 8 * UC
STEP = WIN + 2 * UC
EPS_F = 1e-4
EPS_LN = 1e-5
K6 = 6 * C
NPART = 6 * HD
NE, HID = 8, 384
GC = D + NE
ROW = D + 2
ST = 512
SQ = ST // 128
ETILES = (2 * T + NE * (ST - 1)) // ST
REG = T + ST
SPARE = 8
XROWS = NE * REG + SPARE * ST
YROWS = 2 * T + (NE + SPARE) * ST
ROWS = B * C * NP
STRIP = PATCH * IMG
XT = ROWS // 128
XS = 4
CDQ, CDK = 2 * D, 2 * D + HM
WC = 2 * D + 2 * HM
VH = 6 * C
PL = 96
KCH = 112
Q = 4
QT = NT // Q
QK = T // KCH // Q
ROUNDS = XT // XS
WORK = 11520
XSL = 4
PSL = 4
YSL = 4
GG = 4


def vit_block(nc, x, cw, w_qkv, w_proj, b_proj, proj, wg, w1, b1, w2, b2, out):
    with ExitStack() as ctx:
        def sb(name, shape, dt=F32):
            return ctx.enter_context(nc.sbuf_tensor(name, shape, dt))

        def sem(name):
            return ctx.enter_context(nc.semaphore(name))

        def sems(name, n):
            return [sem(f"{name}{i}") for i in range(n)]

        pooled_d = nc.dram_tensor("pooled_d", [B, C, TOK], F32).ap()
        slots_d = nc.dram_tensor("slots_d", [XROWS, ROW], F32).ap()
        y_d = nc.dram_tensor("y_d", [YROWS, D], F32).ap()

        h2 = sb("h2", [128, NT * GC])
        xt = h2[:, 0:XS * STRIP].rearrange("p (s n) -> p s n", s=XS)
        h2v = h2[0:HT, :].rearrange("p (t n) -> p t n", t=NT)
        us32 = sb("us32", [128, T // 2])
        us = us32[:, :].bitcast(BF16)
        work = sb("work", [128, WORK])

        def carve(at, rows, shape, dt=F32, of=work):
            size = 1
            for n in shape:
                size *= n
            words = (size + 1) // 2 if dt == BF16 else size
            part = of[0:rows, at:at + words]
            if dt != F32:
                part = part.bitcast(dt)
            names = [f"n{i}" for i in range(len(shape))]
            if len(shape) > 1:
                part = part.rearrange(f"p ({' '.join(names)}) -> p {' '.join(names)}",
                                      **dict(zip(names[1:], shape[1:])))
            return part, at + words

        strips = sb("strips", [128, XS, NP])
        ident = sb("ident", [128, 128])
        identb = sb("identb", [128, 128], BF16)
        negib = sb("negib", [128, 128], BF16)
        ones = sb("ones", [128, 128])
        onesb = sb("onesb", [128, 128], BF16)
        trib = sb("trib", [128, 128], BF16)
        epsc = sb("epsc", [128, 2 * TOK])
        ind3 = sb("ind3", [128, HM], BF16)
        umask = sb("umask", [PM, 3, 2, UC])
        vmask = sb("vmask", [NPART, 6])
        cw13 = sb("cw13", [C + 1, D])
        cwc = sb("cwc", [C, D])
        wproj_s = sb("wproj_s", [NPART, 2, GC])
        wvp = sb("wvp", [128, 2, GC])
        gram = sb("gram", [C, C])
        w72 = sb("w72", [128, WC], BF16)
        uu, end = carve(0, HT, [NT, K6], BF16)
        pcr, end = carve(end, C, [T // Q])
        pt, end = carve(XS * STRIP, HT, [NT, C], of=h2)
        gp, end = carve(end, HT, [NT, C], of=h2)
        wall, end = carve(end, C, [WC], of=h2)
        wparts, end = carve(end, C, [3, WC], BF16, of=h2)
        wqkv_s, end = carve(end, NPART, [2, 3 * D], of=h2)
        bd, end = carve(end, NPART, [HALF], of=h2)
        wpt, end = carve(end, NPART, [2, D], of=h2)
        bv, end = carve(end, NPART, [2, 6, C], of=h2)
        cw13t, end = carve(end, NPART, [2, C + 1], of=h2)
        cwct, end = carve(end, NPART, [2, C], of=h2)
        w12t, end = carve(end, NPART, [6, C], of=h2)
        wg_s, end = carve(end, NPART, [2, NE], of=h2)
        wgc, end = carve(end, NPART, [2, NE], of=h2)
        cwm, end = carve(end, C, [2], of=h2)
        cwg, end = carve(end, C + 1, [GC], of=h2)
        assert end <= NT * GC
        var1 = sb("var1", [HT, 6, NT])
        km = sb("km", [KCH, T // KCH])
        kmx = sb("kmx", [128, 3])
        ek, end = carve(0, HT, [2, 2, HM])
        ut = sb("ut", [HT, NT, C])
        u1s = sb("u1s", [HT, 2, 2, 2, UW])
        kuw = sb("kuw", [128, 2, 3 * STEP + 3 * WIN + 2 * UC])
        dk, end = carve(end, HT, [2, 2, NH])
        kut, end = carve(end, 2 * UW, [HALF])
        sq, end = carve(end, HT, [2, 2 * D])
        ss = sb("ss", [HT, 2, 2, 2 * NH])
        qm = sb("qm", [HT, 2, 2, NH])
        shf = sb("shf", [HT, 3, 2, NH])
        s3 = sb("s3", [HT, 2, 3 * NH], BF16)
        sht = sb("sht", [128, TOK], BF16)
        eqt, end = carve(end, 128, [2, PAIRS, TOK])
        rd = sb("rd", [HT, 2, NH])
        at, end = carve(end, HT, [2, 2, NH * C])
        ats = sb("ats", [128, 2, 2, TOK])
        bn = sb("bn", [HT, NT, 6])
        gs, end = carve(0, HT, [NT, NE])
        oh, end = carve(end, HT, [2, NT, NE])
        tmp, end = carve(end, HT, [NT, NE])
        ohb, end = carve(end, HT, [NE, NT], BF16)
        run, end = carve(end, HT, [NE, NT])
        rank, end = carve(end, HT, [NE, NT])
        st, end = carve(end, HT, [10, NT])
        dp, end = carve(end, HT, [NT, 2, 2])
        idx, end = carve(end, HT, [NT, 2])
        hb, end = carve(end, HT, [XSL, 2, ROW])
        hbi, end = carve(end, HT, [XSL, 2], U32)
        assert end <= WORK
        pad, end = carve(0, 128, [PSL, SQ, ROW], of=us32)
        dsti, end = carve(end, 128, [NT, 2], I32, of=us32)
        padi, end = carve(end, 128, [NE + SPARE, SQ], I32, of=us32)
        tab, end = carve(end, 128, [2 * NE + ETILES], I32, of=us32)
        tabf, end = carve(end, 128, [2 * NE + ETILES], of=us32)
        cx, end = carve(end, 128, [8, NE], of=us32)
        tl, end = carve(end, 128, [2, ETILES, NE], of=us32)
        tj, end = carve(end, 128, [2, ETILES], of=us32)
        where = sb("where", [1, 2 * ETILES + NE], I32)
        xin, end = carve(0, 128, [2, SQ, ROW])
        w1t, end = carve(end, NPART, [2, 2, HID])
        w2t, end = carve(end, 128, [2, 3, D])
        b1t, end = carve(end, 128, [2, 3])
        b2t, end = carve(end, 128, [2, D])
        xtr, end = carve(end, NPART, [2, 2, ST])
        hid, end = carve(end, 128, [2, 3, ST])
        ys, end = carve(end, 128, [2, SQ, D])
        ypr, end = carve(end, 128, [2, SQ])
        ydst, end = carve(end, 128, [2, SQ], U32)
        assert end <= WORK
        yin, end = carve(0, HT, [YSL, GG, 2, D])
        assert end <= WORK

        p_kd = ctx.enter_context(nc.psum_tensor("p_kd", [128, 2, 512], F32))
        p_qd = ctx.enter_context(nc.psum_tensor("p_qd", [128, 2, 512], F32))
        p_qk = ctx.enter_context(nc.psum_tensor("p_qk", [128, 512], F32))
        p_m = ctx.enter_context(nc.psum_tensor("p_m", [128, 512], F32))
        p_qt = ctx.enter_context(nc.psum_tensor("p_qt", [128, 2, 512], F32))

        x_in = sems("x_in", XS)
        pooled = sem("pooled")
        strip_out = sems("strip_out", XS)
        w_in = sem("w_in")
        bd_in = sem("bd_in")
        pads = sem("pads")
        cst = sem("cst")
        dz = sem("dz")
        bdz = sem("bdz")
        setup_d = sem("setup_d")
        setup_p = sem("setup_p")
        setup_a = sem("setup_a")
        w72_in = sem("w72_in")
        cwg_in = sem("cwg_in")
        bvm = sem("bvm")
        pc_in = sem("pc_in")
        pc_last = sem("pc_last")
        pt_ps = sem("pt_ps")
        pt_cp = sem("pt_cp")
        ln1 = sem("ln1")
        ln1a = sem("ln1a")
        us_ps = sem("us_ps")
        us_cp = sem("us_cp")
        km_ps = sem("km_ps")
        km_cp = sem("km_cp")
        km_fin = sem("km_fin")
        km_all = sem("km_all")
        stab = sem("stab")
        qk_ready = sem("qk_ready")
        kd_ready = sem("kd_ready")
        qd_ready = sem("qd_ready")
        sq_done = sem("sq_done")
        ek_done = sem("ek_done")
        dk_done = sem("dk_done")
        ss_done = sem("ss_done")
        qm_done = sem("qm_done")
        u1_done = sem("u1_done")
        k1_done = sem("k1_done")
        sh_step = sem("sh_step")
        sh_ps = sem("sh_ps")
        sht_done = sem("sht_done")
        qt_ps = sem("qt_ps")
        eq_done = sem("eq_done")
        kut_ps = sem("kut_ps")
        kut_done = sem("kut_done")
        ku_ps = sem("ku_ps")
        kuw_done = sem("kuw_done")
        eqe_done = sem("eqe_done")
        att_ps = sem("att_ps")
        rd_done = sem("rd_done")
        at_done = sem("at_done")
        ats_done = sem("ats_done")
        g_ps = sem("g_ps")
        h2_done = sem("h2_done")
        bn_done = sem("bn_done")
        pl_in = sems("pl_in", 2)
        sent = sem("sent")
        tables = sem("tables")
        gate_d = sem("gate_d")
        gate_a = sem("gate_a")
        gate_p = sem("gate_p")
        pad_set = sem("pad_set")
        pad_out = sems("pad_out", PSL)
        hb_done = sem("hb_done")
        hb_out = sems("hb_out", XSL)
        begun = sem("begun")
        x_ld = sems("x_ld", 2)
        w_ld = sems("w_ld", 2)
        xt_ps = sem("xt_ps")
        xt_done = sem("xt_done")
        hid_ps = sem("hid_ps")
        hid_done = sem("hid_done")
        ys_ps = sem("ys_ps")
        ys_b = sem("ys_b")
        ypr_done = sem("ypr_done")
        ys_done = sem("ys_done")
        ys_out = sems("ys_out", 2)
        yin_ld = sems("yin_ld", YSL)
        sum0 = sem("sum0")
        sum1 = sem("sum1")
        o_out = sem("o_out")

        x_v = x.rearrange("b c (i k) w -> (b c i) (k w)", k=PATCH).rearrange("(t p) n -> t p n", p=128)
        pooled_v = pooled_d.rearrange("b c (i j) -> (b c i) j", j=NP).rearrange("(t p) j -> t p j", p=128)
        pooled_c = pooled_d.rearrange("b c t -> c b t")

        with nc.Block() as block:

            @block.sync
            def _(sp):
                def load(t, s):
                    sp.dma_start(xt[:, s, :], x_v[bass.ds(t, 1)].rearrange("a p n -> (a p) n"))\
                      .then_inc(x_in[s], 16)

                for s in range(XS):
                    load(s, s)
                with sp.Fori(1, ROUNDS) as i:
                    for s in range(XS):
                        sp.wait_ge(pooled, XS * i + s - XS + 1)
                        load(XS * i + s, s)
                for s in range(XS):
                    sp.wait_ge(strip_out[s], 16 * ROUNDS)

                sp.wait_ge(pt_ps, Q - 1)
                sp.dma_start(pcr[:, :].rearrange("c (b t) -> c b t", b=B // Q), pooled_c[:, B // Q * (Q - 1):, :])\
                  .then_inc(pc_last, 16)

                def load_rows(b, s):
                    sp.dma_start(ats[PL:PL + C, s, 1, :], pooled_d[bass.ds(b, 1)].rearrange("a c t -> (a c) t"))\
                      .then_inc(pl_in[s], 16)

                sp.wait_ge(dz, 6)
                for s in range(2):
                    load_rows(s, s)
                with sp.Fori(1, B // 2) as i:
                    for s in range(2):
                        sp.wait_ge(g_ps, 2 * i + s - 1)
                        load_rows(2 * i + s, s)

            @block.gpsimd
            def _(pool):
                pool.memset(ones[:, :], 1.0).then_inc(cst, 1)
                pool.memset(onesb[:, :], 1.0).then_inc(cst, 1)
                pool.memset(epsc[:, :], EPS_F).then_inc(cst, 1)
                pool.memset(ind3[:, :], 1.0).then_inc(cst, 1)
                pool.memset(umask[:, :, :, :], 1.0).then_inc(cst, 1)
                pool.memset(vmask[:, :], 1.0).then_inc(cst, 1)
                pool.memset(negib[:, :], 0.0).then_inc(cst, 1)
                pool.wait_ge(cst, 7)
                pool.affine_select(out=ident[:, :], in_=ones[:, :], compare_op=ALU.is_equal, fill=0.0,
                                   base=0, pattern=[[-1, 128]], channel_multiplier=1).then_inc(cst, 1)
                pool.affine_select(out=identb[:, :], in_=onesb[:, :], compare_op=ALU.is_equal, fill=0.0,
                                   base=0, pattern=[[-1, 128]], channel_multiplier=1).then_inc(cst, 1)
                pool.affine_select(out=negib[:, :], in_=negib[:, :], compare_op=ALU.not_equal, fill=-1.0,
                                   base=0, pattern=[[-1, 128]], channel_multiplier=1).then_inc(cst, 1)
                pool.affine_select(out=trib[:, :], in_=onesb[:, :], compare_op=ALU.is_gt, fill=0.0,
                                   base=0, pattern=[[1, 128]], channel_multiplier=-1).then_inc(cst, 1)
                for par in range(2):
                    part = umask[:, :, par, :]
                    pool.affine_select(out=part, in_=part, compare_op=ALU.is_gt, fill=0.0,
                                       base=M if par == 0 else 1 - M, pattern=[[0, 3], [0, UC]],
                                       channel_multiplier=-1 if par == 0 else 1).then_inc(cst, 1)
                pool.affine_select(out=vmask[:, :], in_=vmask[:, :], compare_op=ALU.is_ge, fill=0.0,
                                   base=0, pattern=[[-HD, 6]], channel_multiplier=1).then_inc(cst, 1)
                pool.wait_ge(cst, 14)
                pool.affine_select(out=vmask[:, :], in_=vmask[:, :], compare_op=ALU.is_ge, fill=0.0,
                                   base=HD - 1, pattern=[[HD, 6]], channel_multiplier=-1).then_inc(cst, 1)
                pool.affine_select(out=ind3[:, :].rearrange("p (h m) -> p h m", h=NH),
                                   in_=ind3[:, :].rearrange("p (h m) -> p h m", h=NH),
                                   compare_op=ALU.is_equal, fill=2.0, base=0,
                                   pattern=[[-1, NH], [0, M]], channel_multiplier=1).then_inc(cst, 1)
                pool.wait_ge(cst, 16)
                pool.affine_select(out=ind3[:, :].rearrange("p (h m) -> p h m", h=NH),
                                   in_=ind3[:, :].rearrange("p (h m) -> p h m", h=NH),
                                   compare_op=ALU.not_equal, fill=1.0, base=-NH,
                                   pattern=[[-1, NH], [0, M]], channel_multiplier=1).then_inc(cst, 1)
                pool.wait_ge(cst, 17)
                pool.affine_select(out=ind3[:, :].rearrange("p (h m) -> p h m", h=NH),
                                   in_=ind3[:, :].rearrange("p (h m) -> p h m", h=NH),
                                   compare_op=ALU.not_equal, fill=1.0, base=-2 * NH,
                                   pattern=[[-1, NH], [0, M]], channel_multiplier=1).then_inc(cst, 1)
                pool.wait_ge(cst, 18)
                pool.tensor_scalar(ind3[:, :], ind3[:, :], 1.0, None, ALU.is_equal).then_inc(cst, 1)

                for q in range(Q - 1):
                    for s in range(XS):
                        pool.wait_ge(strip_out[s], 16 * (5 * q + 6))
                    if q > 0:
                        pool.wait_ge(pt_ps, q)
                    pool.dma_start(pcr[:, :].rearrange("c (b t) -> c b t", b=B // Q),
                                   pooled_c[:, B // Q * q:B // Q * (q + 1), :]).then_inc(pc_in, 16)

                pool.wait_ge(km_fin, 1)
                pool.partition_all_reduce(kmx[0:KCH, 1:2], kmx[0:KCH, 0:1], KCH, bass.bass_isa.ReduceOp.max)\
                    .then_inc(km_all, 1)

                def key_features(b, s, t):
                    pool.wait_ge(dk_done, 2 * b + t + 1)
                    e = ek[:, s, t, :].rearrange("p (h m) -> p h m", m=M)
                    pool.tensor_tensor(e, e, dk[:, s, t, :].unsqueeze(2).to_broadcast([HT, NH, M]), ALU.mult)\
                        .then_inc(k1_done, 1)

                for t in range(2):
                    key_features(0, 0, t)

                def image(b, s):
                    for t in range(2):
                        key_features(b + 1, 1 - s, t)

                with pool.Fori(0, B // 2 - 1) as i:
                    image(2 * i, 0)
                    image(2 * i + 1, 1)
                image(B - 2, 0)

            @block.scalar
            def _(act):
                def first_stores():
                    for s in range(XS):
                        act.wait_ge(pooled, s + 1)
                        act.dma_start(pooled_v[s], strips[:, s, :]).then_inc(strip_out[s], 16)

                act.dma_start(cw13[0:C, :], cw).then_inc(w_in, 16)
                act.dma_start(cw13[C:C + 1, :], b_proj.rearrange("(a n) -> a n", a=1)).then_inc(w_in, 16)
                act.dma_start(wqkv_s[:, :, :], w_qkv.rearrange("(c p) n -> p c n", p=NPART)).then_inc(w_in, 16)
                act.dma_start(wproj_s[:, :, 0:D], w_proj.rearrange("(c p) n -> p c n", p=NPART)).then_inc(w_in, 16)
                act.dma_start(wg_s[:, :, :], wg.rearrange("(c p) n -> p c n", p=NPART)).then_inc(w_in, 16)
                act.wait_ge(bdz, 1)
                for h in range(6):
                    act.dma_start(bd[HD * h:HD * h + HD, M * h:M * h + M], proj.rearrange("m d -> d m"),
                                  allow_slow_non_contiguous=True)\
                       .then_inc(bd_in, 16)

                first_stores()
                act.wait_ge(setup_p, 1)
                act.copy(cwct[:, :, :], p_m[0:NPART, 0:2 * C].rearrange("p (c n) -> p c n", c=2)).then_inc(setup_a, 1)
                act.copy(cw13t[:, :, :], p_m[0:NPART, 32:32 + 2 * (C + 1)].rearrange("p (c n) -> p c n", c=2))\
                   .then_inc(setup_a, 1)
                act.copy(wpt[:, :, :], p_m[0:NPART, 64:64 + 2 * D].rearrange("p (c n) -> p c n", c=2)).then_inc(setup_a, 1)
                act.wait_ge(setup_p, 2)
                act.copy(wall[:, 0:2 * D], p_kd[0:C, 0, 0:2 * D]).then_inc(setup_a, 1)
                act.copy(w12t[:, :, :], p_qd[0:NPART, 0, 0:6 * C].rearrange("p (c n) -> p c n", c=6)).then_inc(setup_a, 1)
                act.mul(gram[:, :], p_qd[0:C, 1, 0:C], 1.0 / D).then_inc(setup_a, 1)
                act.copy(cwg[:, D:GC], p_qk[0:C + 1, 0:NE]).then_inc(setup_a, 1)
                for g in range(2):
                    act.copy(wproj_s[:, g, D:GC], p_qk[0:NPART, 16 + 16 * g:16 + 16 * g + NE]).then_inc(setup_a, 1)
                act.wait_ge(w_in, 80)
                act.copy(cwg[:, 0:D], cw13[:, :]).then_inc(setup_a, 1)
                act.wait_ge(setup_a, 10)
                act.wait_ge(dz, 6)
                act.dma_start(wvp[PL:PL + C + 1, 1, :], cwg[:, :]).then_inc(cwg_in, 16)
                act.wait_ge(setup_p, 3)
                for g in range(4):
                    src = (p_kd, p_kd, p_qt, p_qt)[g]
                    act.mul(wall[:, CDQ + HALF * g:CDQ + HALF * g + HALF], src[0:C, g % 2, 0:HALF], 0.5)\
                       .then_inc(setup_a, 1)
                for g in range(2):
                    act.copy(wvp[0:VH, g, :], p_m[0:VH, GC * g:GC * g + GC]).then_inc(setup_a, 1)
                act.wait_ge(setup_d, 7)
                for r, part in enumerate((0, 1, 2, 0, 1, 0)):
                    if r == 0:
                        act.wait_ge(pads, 2)
                    act.dma_start(w72[C * r:C * r + C, :], wparts[:, part, :]).then_inc(w72_in, 16)

                def store(i):
                    for s in range(XS):
                        act.wait_ge(pooled, XS * i + s + 1)
                        act.dma_start(pooled_v[bass.ds(XS * i + s, 1)].rearrange("a p j -> (a p) j"),
                                      strips[:, s, :]).then_inc(strip_out[s], 16)

                def token_rows(q):
                    act.wait_ge(pt_ps, q + 1)
                    act.copy(pt[:, bass.ds(QT * q, QT), :], p_m[0:HT, 0:QT * C].rearrange("p (t c) -> p t c", t=QT))\
                       .then_inc(pt_cp, 1)
                    act.copy(gp[:, bass.ds(QT * q, QT), :], p_qk[0:HT, 0:QT * C].rearrange("p (t c) -> p t c", t=QT))\
                       .then_inc(pt_cp, 1)

                def split(q):
                    t = bass.ds(QT * q, QT)
                    act.wait_ge(ln1, 13 * q + 3)
                    act.activation(var1[:, 1, t], var1[:, 0, t], ACT.Sqrt).then_inc(ln1a, 1)
                    act.wait_ge(ln1, 13 * q + 10)
                    act.copy(uu[:, t, C:2 * C], uu[:, t, 0:C]).then_inc(ln1a, 1)
                    act.copy(uu[:, t, 2 * C:3 * C], uu[:, t, 0:C]).then_inc(ln1a, 1)
                    act.wait_ge(ln1, 13 * q + 12)
                    act.copy(uu[:, t, 4 * C:5 * C], uu[:, t, 3 * C:4 * C]).then_inc(ln1a, 1)
                    for g in range(QT // GG):
                        n = QT // GG * q + g
                        act.wait_ge(us_ps, n + 1)
                        act.copy(us[0:K6, bass.ds(n * GG * HT, GG * HT)], p_kd[0:K6, g % 2, 0:GG * HT])\
                           .then_inc(us_cp, 1)

                with act.Fori(1, 6) as i:
                    store(i)
                with act.Fori(0, Q - 1) as q:
                    store(5 * q + 6)
                    store(5 * q + 7)
                    token_rows(q)
                    split(q)
                    for r in range(3):
                        store(5 * q + 8 + r)
                token_rows(Q - 1)
                split(Q - 1)

                act.wait_ge(km_all, 1)
                act.mul(kmx[0:KCH, 2:3], kmx[0:KCH, 1:2], -1.0).then_inc(stab, 1)
                act.wait_ge(stab, 1)

                def front(b, s, t, first=False, turn=None):
                    n = 2 * b + t
                    act.wait_ge(qk_ready, n + 1)
                    if not (first):
                        act.wait_ge(ss_done, n - 1)
                    act.activation(sq[:, t, :], p_qk[0:HT, 0:2 * D], ACT.Square).then_inc(sq_done, 1)
                    act.wait_ge(kd_ready, n + 1)
                    act.activation(ek[:, s, t, :].rearrange("p (g n) -> p g n", g=2), p_kd[0:HT, :, 0:HALF],
                                   ACT.Exp, bias=kmx[0:HT, 2:3]).then_inc(ek_done, 1)
                    if turn is not None:
                        turned(*turn)
                    act.wait_ge(ss_done, n + 1)
                    act.activation(dk[:, s, t, :], ss[:, s, t, NH:2 * NH], ACT.Exp, scale=-0.125)\
                       .then_inc(dk_done, 1)

                def tokens(b, s):
                    act.copy(u1s[:, s, :, :, 0:C], ut[:, bass.ds(2 * b, 2), :].unsqueeze(2)
                             .to_broadcast([HT, 2, 2, C])).then_inc(u1_done, 1)

                def query_exp(b, s, r):
                    act.wait_ge(qt_ps, 3 * b + r + 1)
                    act.activation(eqt[0:PM, s, 2 * r:2 * r + 2, :],
                                   p_qt[0:PM, r % 2, 0:2 * TOK].rearrange("p (a t) -> p a t", a=2),
                                   ACT.Exp).then_inc(eq_done, 1)

                def query_eps(b, s, r):
                    act.wait_ge(eq_done, 3 * b + r + 1)
                    act.activation(eqt[0:PM, s, 2 * r:2 * r + 2, :], eqt[0:PM, s, 2 * r:2 * r + 2, :], ACT.Identity,
                                   bias=epsc[0:PM, 0:1]).then_inc(eqe_done, 1)

                def turned(b, s):
                    if not (isinstance(b, int) and b < 2):
                        act.wait_ge(g_ps, b - 1)
                    act.copy(ats[0:VH, s, :, :], p_kd[0:VH, :, HALF:HALF + TOK]).then_inc(ats_done, 1)

                def rows(b):
                    act.wait_ge(g_ps, b + 1)
                    act.copy(h2v[:, bass.ds(2 * b, 2), :], p_m[0:HT, 0:2 * GC].rearrange("p (t n) -> p t n", t=2))\
                       .then_inc(h2_done, 1)

                act.wait_ge(pads, 4)
                tokens(0, 0)
                front(0, 0, 0, first=True)
                front(0, 0, 1, first=True)

                def image(b, s, first=False, more=True):
                    if more:
                        if not (isinstance(b, int) and b == 0):
                            act.wait_ge(kut_ps, b)
                        tokens(b + 1, 1 - s)
                        front(b + 1, 1 - s, 0)
                    if not (isinstance(b, int) and b < 2):
                        act.wait_ge(att_ps, b - 1)
                    query_exp(b, s, 0)
                    query_exp(b, s, 1)
                    if more:
                        front(b + 1, 1 - s, 1, turn=None if first else (b - 1, 1 - s))
                    else:
                        act.wait_ge(kd_ready, 2 * B + 1)
                        turned(b - 1, 1 - s)
                    query_eps(b, s, 0)
                    query_eps(b, s, 1)
                    query_exp(b, s, 2)
                    query_eps(b, s, 2)
                    if not first:
                        rows(b - 1)

                image(0, 0, first=True)
                image(1, 1)
                image(2, 0)
                image(3, 1)
                with act.Fori(2, B // 2 - 1) as i:
                    image(2 * i, 0)
                    image(2 * i + 1, 1)
                image(B - 2, 0)
                image(B - 1, 1, more=False)
                act.wait_ge(kd_ready, 2 * B + 2)
                turned(B - 1, 1)
                rows(B - 1)

            @block.vector
            def _(dve):
                dve.memset(bd[:, :], 0.0).then_inc(bdz, 1)
                dve.memset(us[64:128, :], 0.0).then_inc(pads, 1)
                def pool_tiles(i, first=False):
                    for s in range(XS):
                        dve.wait_ge(x_in[s], 16 * i + 16)
                        if not first:
                            dve.wait_ge(strip_out[s], 16 * i)
                        dve.tensor_reduce(strips[:, s, :],
                                          xt[:, s, :].rearrange("p (k j l) -> p j k l", k=PATCH, l=PATCH),
                                          AX.XY, ALU.add).then_inc(pooled, 1)

                pool_tiles(0, first=True)
                dve.wait_ge(w_in, 80)
                dve.reduce_sum(cwm[:, 0:1], cw13[0:C, :], axis=AX.X).then_inc(setup_d, 1)
                dve.wait_ge(setup_d, 1)
                dve.tensor_scalar(cwm[:, 1:2], cwm[:, 0:1], 1.0 / D, None, ALU.mult).then_inc(setup_d, 1)
                dve.wait_ge(setup_d, 2)
                dve.tensor_scalar(cwc[:, :], cw13[0:C, :], cwm[:, 1:2], None, ALU.subtract).then_inc(setup_d, 1)
                dve.memset(u1s[:, :, :, :, :], 0.0).then_inc(bvm, 1)
                dve.memset(w72[:, :], 0.0).then_inc(pads, 1)
                dve.memset(sht[:, :], 0.0).then_inc(pads, 1)
                dve.memset(kuw[:, :, :], 0.0).then_inc(dz, 1)
                dve.memset(wvp[:, :, :], 0.0).then_inc(dz, 1)
                dve.memset(ats[64:96, :, :, :], 0.0).then_inc(dz, 1)
                dve.memset(ats[96:128, :, :, :], 1.0).then_inc(dz, 1)
                dve.wait_ge(bvm, 1)
                dve.memset(u1s[:, :, :, :, C:UC], 1.0).then_inc(bvm, 1)
                dve.wait_ge(setup_p, 1)
                for c in range(2):
                    dve.scalar_tensor_tensor(out=wgc[:, c, :], in0=p_qt[0:NPART, 0, 0:NE], scalar=-1.0 / D,
                                             in1=wg_s[:, c, :], op0=ALU.mult, op1=ALU.add).then_inc(dz, 1)
                dve.wait_ge(setup_a, 10)
                for g in range(2):
                    dve.tensor_tensor(bv[:, g, :, :], w12t[:, 4 + g, :].unsqueeze(1).to_broadcast([NPART, 6, C]),
                                      vmask[:, :].unsqueeze(2).to_broadcast([NPART, 6, C]), ALU.mult).then_inc(bvm, 1)
                dve.wait_ge(setup_a, 14)
                dve.tensor_copy(wparts[:, 0, :], wall[:, :]).then_inc(setup_d, 1)
                dve.wait_ge(setup_d, 4)
                dve.tensor_tensor(wall[:, :], wall[:, :], wparts[:, 0, :], ALU.subtract).then_inc(setup_d, 1)
                dve.wait_ge(setup_d, 5)
                dve.tensor_copy(wparts[:, 1, :], wall[:, :]).then_inc(setup_d, 1)
                dve.wait_ge(setup_d, 6)
                dve.tensor_tensor(wparts[:, 2, :], wall[:, :], wparts[:, 1, :], ALU.subtract).then_inc(setup_d, 1)

                def normalise(q):
                    o = 13 * q
                    t = bass.ds(QT * q, QT)
                    dve.wait_ge(pt_cp, 2 * q + 2)
                    dve.tensor_tensor(gp[:, t, :], gp[:, t, :], pt[:, t, :], ALU.mult).then_inc(ln1, 1)
                    dve.wait_ge(ln1, o + 1)
                    dve.tensor_reduce(var1[:, 5, t], gp[:, t, :], AX.X, ALU.add).then_inc(ln1, 1)
                    dve.wait_ge(ln1, o + 2)
                    dve.tensor_scalar(var1[:, 0, t], var1[:, 5, t], EPS_LN, None, ALU.add).then_inc(ln1, 1)
                    dve.wait_ge(ln1a, 4 * q + 1)
                    dve.reciprocal(var1[:, 2, t], var1[:, 1, t]).then_inc(ln1, 1)
                    dve.wait_ge(ln1, o + 4)
                    dve.tensor_tensor(var1[:, 3, t], var1[:, 2, t], var1[:, 2, t], ALU.mult).then_inc(ln1, 1)
                    dve.wait_ge(ln1, o + 5)
                    dve.tensor_tensor(var1[:, 4, t], var1[:, 3, t], var1[:, 0, t], ALU.mult).then_inc(ln1, 1)
                    dve.wait_ge(ln1, o + 6)
                    dve.tensor_scalar(var1[:, 3, t], var1[:, 4, t], -0.5, 1.5, ALU.mult, ALU.add).then_inc(ln1, 1)
                    dve.wait_ge(ln1, o + 7)
                    dve.tensor_tensor(var1[:, 5, t], var1[:, 3, t], var1[:, 2, t], ALU.mult).then_inc(ln1, 1)
                    dve.wait_ge(ln1, o + 8)
                    dve.tensor_tensor(ut[:, t, :], pt[:, t, :], var1[:, 5, t].unsqueeze(2).to_broadcast([HT, QT, C]),
                                      ALU.mult).then_inc(ln1, 1)
                    dve.wait_ge(ln1, o + 9)
                    dve.tensor_copy(uu[:, t, 0:C], ut[:, t, :]).then_inc(ln1, 1)
                    dve.wait_ge(ln1, o + 10)
                    dve.tensor_tensor(gp[:, t, :], ut[:, t, :], uu[:, t, 0:C], ALU.subtract).then_inc(ln1, 1)
                    dve.wait_ge(ln1, o + 11)
                    dve.tensor_copy(uu[:, t, 3 * C:4 * C], gp[:, t, :]).then_inc(ln1, 1)
                    dve.wait_ge(ln1, o + 12)
                    dve.tensor_tensor(uu[:, t, 5 * C:6 * C], gp[:, t, :], uu[:, t, 3 * C:4 * C], ALU.subtract)\
                       .then_inc(ln1, 1)

                def key_max(q):
                    for n in range(QK):
                        src = (p_kd, p_qd)[n % 2]
                        dve.wait_ge(km_ps, QK * q + n + 1)
                        dve.tensor_reduce(km[:, bass.ds(QK * q + n, 1)], src[0:KCH, :, 0:HALF], AX.XY, ALU.max)\
                           .then_inc(km_cp, 1)

                with dve.Fori(1, 6) as i:
                    pool_tiles(i)
                with dve.Fori(0, Q - 1) as q:
                    pool_tiles(5 * q + 6)
                    pool_tiles(5 * q + 7)
                    normalise(q)
                    pool_tiles(5 * q + 8)
                    key_max(q)
                    pool_tiles(5 * q + 9)
                    pool_tiles(5 * q + 10)
                normalise(Q - 1)
                key_max(Q - 1)
                dve.wait_ge(km_cp, T // KCH)
                dve.tensor_reduce(kmx[0:KCH, 0:1], km[:, :], AX.X, ALU.max).then_inc(km_fin, 1)

                dve.wait_ge(us_cp, NT // GG)
                dve.memset(eqt[64:128, :, :, :], 0.0).then_inc(pads, 1)

                def squares(b, s, t):
                    dve.wait_ge(sq_done, 2 * b + t + 1)
                    dve.tensor_reduce(ss[:, s, t, :], sq[:, t, :].rearrange("p (h d) -> p h d", d=HD), AX.X, ALU.add)\
                       .then_inc(ss_done, 1)

                def query_max(b, s, t):
                    dve.wait_ge(qd_ready, 2 * b + t + 1)
                    dve.tensor_reduce(qm[:, s, t, :].rearrange("p (g h) -> p g h", g=2),
                                      p_qd[0:HT, :, 0:HALF].rearrange("p g (h m) -> p g h m", m=M),
                                      AX.X, ALU.max).then_inc(qm_done, 1)

                def shift(b, s):
                    dve.wait_ge(ss_done, 2 * b + 2)
                    dve.wait_ge(qm_done, 2 * b + 2)
                    if not (isinstance(b, int) and b == 0):
                        dve.wait_ge(sh_ps, b)
                    dve.scalar_tensor_tensor(out=shf[:, 0], in0=ss[:, s, :, 0:NH], scalar=0.125, in1=qm[:, s],
                                             op0=ALU.mult, op1=ALU.add).then_inc(sh_step, 1)
                    dve.wait_ge(sh_step, 6 * b + 1)
                    dve.tensor_copy(s3[:, :, 0:NH], shf[:, 0]).then_inc(sh_step, 1)
                    dve.wait_ge(sh_step, 6 * b + 2)
                    dve.tensor_tensor(shf[:, 1], shf[:, 0], s3[:, :, 0:NH], ALU.subtract).then_inc(sh_step, 1)
                    dve.wait_ge(sh_step, 6 * b + 3)
                    dve.tensor_copy(s3[:, :, NH:2 * NH], shf[:, 1]).then_inc(sh_step, 1)
                    dve.wait_ge(sh_step, 6 * b + 4)
                    dve.tensor_tensor(shf[:, 2], shf[:, 1], s3[:, :, NH:2 * NH], ALU.subtract).then_inc(sh_step, 1)
                    dve.wait_ge(sh_step, 6 * b + 5)
                    dve.tensor_copy(s3[:, :, 2 * NH:3 * NH], shf[:, 2]).then_inc(sh_step, 1)

                def spread(b, s):
                    if not (isinstance(b, int) and b < 2):
                        dve.wait_ge(att_ps, b - 1)
                    dve.wait_ge(ku_ps, b + 1)
                    for g in range(2):
                        at0 = g * (3 * WIN + 2 * UC)
                        src = p_m[0:PM, 0:3 * 2 * UW].rearrange("p (a g c) -> p a g c", a=3, g=2)[:, :, g, 0:UC]
                        dve.tensor_tensor(
                            kuw[0:PM, s, at0:at0 + 3 * STEP].rearrange("p (a w) -> p a w", a=3)[:, :, 0:2 * UC]
                            .rearrange("p a (e c) -> p a e c", e=2),
                            src.unsqueeze(2).to_broadcast([PM, 3, 2, UC]), umask[:, :, :, :], ALU.mult)\
                           .then_inc(kuw_done, 1)

                def statistics(b):
                    dve.wait_ge(h2_done, b + 1)
                    for t in range(2):
                        dve.bn_stats(bn[:, bass.ds(2 * b + t, 1), :].rearrange("p a n -> p (a n)"),
                                     h2v[:, bass.ds(2 * b + t, 1), 0:D].rearrange("p a n -> p (a n)"))\
                           .then_inc(bn_done, 1)

                def shifted(b):
                    dve.wait_ge(sh_ps, b + 1)
                    dve.tensor_copy(sht[0:3 * NH, :], p_qd[0:3 * NH, 0, HALF:HALF + TOK]).then_inc(sht_done, 1)

                for t in range(2):
                    squares(0, 0, t)
                    query_max(0, 0, t)
                shift(0, 0)
                shifted(0)

                def image(b, s, first=False, more=True):
                    if more:
                        squares(b + 1, 1 - s, 0)
                        query_max(b + 1, 1 - s, 0)
                    dve.wait_ge(kut_ps, b + 1)
                    dve.tensor_scalar(kut[:, :], p_m[0:2 * UW, 0:HALF], p_m[0:2 * UW, HALF:HALF + 1], None, ALU.add)\
                       .then_inc(kut_done, 1)
                    if more:
                        squares(b + 1, 1 - s, 1)
                    spread(b, s)
                    if more:
                        query_max(b + 1, 1 - s, 1)
                        shift(b + 1, 1 - s)
                        shifted(b + 1)
                    if not first:
                        statistics(b - 1)
                    dve.wait_ge(att_ps, b + 1)
                    a = p_qt[0:HT, 1, 0:2 * NH * UC].rearrange("p (t h c) -> p t h c", t=2, c=UC)
                    dve.reciprocal(rd[:, :, :], a[:, :, :, C]).then_inc(rd_done, 1)
                    dve.wait_ge(rd_done, b + 1)
                    for t in range(2):
                        dve.tensor_tensor(at[:, s, t, :].rearrange("p (h d) -> p h d", d=C), a[:, t, :, 0:C],
                                          rd[:, t, :].unsqueeze(2).to_broadcast([HT, NH, C]), ALU.mult)\
                           .then_inc(at_done, 1)

                image(0, 0, first=True)
                image(1, 1)
                image(2, 0)
                image(3, 1)
                with dve.Fori(2, B // 2 - 1) as i:
                    image(2 * i, 0)
                    image(2 * i + 1, 1)
                image(B - 2, 0)
                image(B - 1, 1, more=False)
                statistics(B - 1)

            @block.tensor
            def _(pe):
                pe.wait_ge(cst, 19)
                pe.wait_ge(setup_d, 3)
                for c in range(2):
                    cols = slice(NPART * c, NPART * c + NPART)
                    pe.transpose(p_m[0:NPART, C * c:C * c + C], cwc[:, cols], ident[0:C, 0:C])
                    pe.transpose(p_m[0:NPART, 32 + (C + 1) * c:32 + (C + 1) * (c + 1)], cw13[:, cols],
                                 ident[0:C + 1, 0:C + 1])
                    for g in range(2):
                        pe.transpose(p_m[0:NPART, 64 + D * c + NPART * g:64 + D * c + NPART * (g + 1)],
                                     wproj_s[:, g, cols], ident[0:NPART, 0:NPART])
                for c in range(2):
                    mm = pe.matmul(p_qt[0:NPART, 0, 0:NE], ones[0:NPART, 0:NPART], wg_s[:, c, :],
                                   start=(c == 0), stop=(c == 1))
                mm.then_inc(setup_p, 1)
                pe.wait_ge(setup_a, 3)
                pe.wait_ge(dz, 6)
                for c in range(2):
                    pe.matmul(p_kd[0:C, 0, 0:2 * D], cwct[:, c, :], wqkv_s[:, c, 0:2 * D], start=(c == 0), stop=(c == 1))
                for g in range(6):
                    for c in range(2):
                        pe.matmul(p_qd[0:NPART, 0, C * g:C * g + C], wqkv_s[:, c, NPART * g:NPART * g + NPART],
                                  cwct[:, c, :], start=(c == 0), stop=(c == 1))
                for c in range(2):
                    pe.matmul(p_qd[0:C, 1, 0:C], cwct[:, c, :], cwct[:, c, :], start=(c == 0), stop=(c == 1))
                for c in range(2):
                    pe.matmul(p_qk[0:C + 1, 0:NE], cw13t[:, c, :], wgc[:, c, :], start=(c == 0), stop=(c == 1))
                for g in range(2):
                    for c in range(2):
                        mm = pe.matmul(p_qk[0:NPART, 16 + 16 * g:16 + 16 * g + NE], wpt[:, c, NPART * g:NPART * g + NPART],
                                       wgc[:, c, :], start=(c == 0), stop=(c == 1))
                mm.then_inc(setup_p, 1)
                pe.wait_ge(setup_a, 10)
                pe.wait_ge(bd_in, 96)
                pe.wait_ge(bvm, 4)
                for g in range(2):
                    pe.matmul(p_m[0:VH, GC * g:GC * g + GC], bv[:, g, :, :].rearrange("p h c -> p (h c)"),
                              wproj_s[:, g, :], start=True, stop=True)
                for g in range(4):
                    dst = (p_kd, p_kd, p_qt, p_qt)[g]
                    mm = pe.matmul(dst[0:C, g % 2, 0:HALF], w12t[:, g, :], bd[:, :], start=True, stop=True)
                mm.then_inc(setup_p, 1)

                pe.wait_ge(setup_a, 16)
                pe.wait_ge(w72_in, 96)

                def part(q):
                    if isinstance(q, int):
                        pe.wait_ge(pc_last, 16)
                    else:
                        pe.wait_ge(pc_in, 16 * q + 16)
                    for t in range(QT):
                        pe.matmul(p_qk[0:HT, C * t:C * t + C], pcr[:, HT * t:HT * t + HT], gram[:, :],
                                  start=True, stop=True)
                    for t in range(QT):
                        mm = pe.transpose(p_m[0:HT, C * t:C * t + C], pcr[:, HT * t:HT * t + HT], ident[0:C, 0:C])
                    mm.then_inc(pt_ps, 1)
                    pe.wait_ge(ln1, 13 * q + 13)
                    pe.wait_ge(ln1a, 4 * q + 4)
                    for g in range(QT // GG):
                        if g > 1:
                            pe.wait_ge(us_cp, QT // GG * q + g - 1)
                        for t in range(GG):
                            mm = pe.matmul(p_kd[0:K6, g % 2, HT * t:HT * t + HT],
                                           uu[:, bass.ds(QT * q + GG * g + t, 1), :].rearrange("p a n -> p (a n)"),
                                           identb[0:HT, 0:HT], start=True, stop=True)
                        mm.then_inc(us_ps, 1)
                    pe.wait_ge(us_cp, QT // GG * (q + 1))
                    for n in range(QK):
                        dst = (p_kd, p_qd)[n % 2]
                        if n > 1:
                            pe.wait_ge(km_cp, QK * q + n - 1)
                        for g in range(2):
                            mm = pe.matmul(dst[0:KCH, g, 0:HALF], us[:, bass.ds(KCH * (QK * q + n), KCH)],
                                           w72[:, CDK + HALF * g:CDK + HALF * g + HALF], start=True, stop=True)
                        mm.then_inc(km_ps, 1)

                with pe.Fori(0, Q - 1) as q:
                    part(q)
                part(Q - 1)
                pe.wait_ge(km_cp, T // KCH)

                def front(b, t, turned=None):
                    n = 2 * b + t
                    u = us[:, bass.ds(TOK * b + HT * t, HT)]
                    fresh = isinstance(b, int) and b == 0 and t == 0
                    if not fresh:
                        pe.wait_ge(sq_done, n)
                    pe.matmul(p_qk[0:HT, 0:2 * D], u, w72[:, 0:2 * D], start=True, stop=True).then_inc(qk_ready, 1)
                    if not fresh:
                        pe.wait_ge(ek_done, n)
                    if t == 0 and not (isinstance(b, int) and b < 3):
                        pe.wait_ge(ats_done, b - 2)
                    for g in range(2):
                        mm = pe.matmul(p_kd[0:HT, g, 0:HALF], u, w72[:, CDK + HALF * g:CDK + HALF * g + HALF],
                                  start=True, stop=True)
                    if turned is not None:
                        mm = turn_rows(*turned)
                    mm.then_inc(kd_ready, 1)
                    if not fresh:
                        pe.wait_ge(qm_done, n)
                        if t == 0:
                            pe.wait_ge(sht_done, b)
                    for g in range(2):
                        mm = pe.matmul(p_qd[0:HT, g, 0:HALF], u, w72[:, CDQ + HALF * g:CDQ + HALF * g + HALF],
                                       start=True, stop=True)
                    mm.then_inc(qd_ready, 1)

                def turn_rows(b, s):
                    pe.wait_ge(at_done, 2 * b + 2)
                    for t in range(2):
                        for g in range(2):
                            mm = pe.transpose(p_kd[0:VH, g, HALF + HT * t:HALF + HT * t + HT],
                                              at[:, s, t, VH * g:VH * g + VH], ident[0:HT, 0:HT])
                    return mm

                def queries(b, s, r):
                    u = us[:, bass.ds(TOK * b, TOK)]
                    for a in range(2):
                        p = 2 * r + a
                        pe.matmul(p_qt[0:PM, r % 2, TOK * a:TOK * a + TOK], w72[:, CDQ + PM * p:CDQ + PM * p + PM], u,
                                  start=True, stop=False)
                        mm = pe.matmul(p_qt[0:PM, r % 2, TOK * a:TOK * a + TOK], ind3[:, PM * p:PM * p + PM], sht[:, :],
                                       start=False, stop=True)
                    mm.then_inc(qt_ps, 1)

                def channel_keys(b, s):
                    pe.wait_ge(k1_done, 2 * b + 2)
                    pe.wait_ge(u1_done, b + 1)
                    for g in range(2):
                        for t in range(2):
                            pe.matmul(p_m[UW * g:UW * g + UW, 0:HALF], u1s[:, s, t, g, :],
                                      ek[:, s, t, HALF * g:HALF * g + HALF], start=(t == 0), stop=(t == 1))
                    for t in range(2):
                        mm = pe.matmul(p_m[0:2 * UW, HALF:HALF + 1], u1s[:, s, t, :, :].rearrange("p g c -> p (g c)"),
                                       epsc[0:HT, 0:1], start=(t == 0), stop=(t == 1))
                    mm.then_inc(kut_ps, 1)

                def key_channels(b):
                    pe.wait_ge(cst, 19)
                    pe.wait_ge(kut_done, b + 1)
                    for a in range(3):
                        mm = pe.transpose(p_m[0:PM, 2 * UW * a:2 * UW * (a + 1)], kut[:, PM * a:PM * a + PM],
                                          ident[0:2 * UW, 0:2 * UW])
                    mm.then_inc(ku_ps, 1)

                def attend(b, s):
                    pe.wait_ge(kuw_done, 2 * b + 2)
                    pe.wait_ge(eqe_done, 3 * b + 3)
                    for t in range(2):
                        for p in range(PAIRS):
                            col = NH * UC * t + (0 if p < 3 else 4 * UC)
                            mm = pe.matmul(p_qt[0:HT, 1, col:col + WIN], eqt[:, s, p, HT * t:HT * t + HT],
                                           kuw[:, s, WIN * p:WIN * p + WIN], start=(p == 0), stop=(p == PAIRS - 1),
                                           skip_group_check=True)
                    mm.then_inc(att_ps, 1)

                def project(b, s):
                    pe.wait_ge(ats_done, b + 1)
                    pe.wait_ge(pl_in[s], 8 * (b - s) + 16)
                    for t in range(2):
                        pe.matmul(p_m[0:HT, GC * t:GC * t + GC], ats[:, s, 0, HT * t:HT * t + HT], wvp[:, 0, :],
                                  start=True, stop=False)
                        mm = pe.matmul(p_m[0:HT, GC * t:GC * t + GC], ats[:, s, 1, HT * t:HT * t + HT],
                                       wvp[:, 1, :], start=False, stop=True)
                    mm.then_inc(g_ps, 1)

                def turn_shift(b):
                    pe.wait_ge(sh_step, 6 * b + 6)
                    for t in range(2):
                        mm = pe.matmul(p_qd[0:3 * NH, 0, HALF + HT * t:HALF + HT * t + HT], s3[:, t, :],
                                       negib[0:HT, 0:HT], start=True, stop=True)
                    mm.then_inc(sh_ps, 1)

                pe.wait_ge(cwg_in, 16)
                front(0, 0)
                front(0, 1)
                turn_shift(0)

                def image(b, s, first=False, more=True):
                    if more:
                        front(b + 1, 0)
                    pe.wait_ge(sht_done, b + 1)
                    if not first:
                        pe.wait_ge(eq_done, 3 * b)
                    queries(b, s, 0)
                    if not first and not (isinstance(b, int) and b < 2):
                        pe.wait_ge(h2_done, b - 1)
                    channel_keys(b, s)
                    if not first:
                        pe.wait_ge(at_done, 2 * b)
                    queries(b, s, 1)
                    if more:
                        front(b + 1, 1, None if first else (b - 1, 1 - s))
                    else:
                        pe.wait_ge(ek_done, 2 * B)
                        pe.wait_ge(ats_done, b - 1)
                        turn_rows(b - 1, 1 - s).then_inc(kd_ready, 1)
                    key_channels(b)
                    pe.wait_ge(eq_done, 3 * b + 1)
                    queries(b, s, 2)
                    if not first:
                        pe.wait_ge(kuw_done, 2 * b + 2)
                        project(b - 1, 1 - s)
                    if more:
                        turn_shift(b + 1)
                    attend(b, s)

                image(0, 0, first=True)
                image(1, 1)
                image(2, 0)
                image(3, 1)
                with pe.Fori(2, B // 2 - 1) as i:
                    image(2 * i, 0)
                    image(2 * i + 1, 1)
                image(B - 2, 0)
                image(B - 1, 1, more=False)
                pe.wait_ge(ats_done, B - 1)
                turn_rows(B - 1, 1).then_inc(kd_ready, 1)
                pe.wait_ge(h2_done, B - 1)
                project(B - 1, 1)

        with nc.Block() as block:

            @block.gpsimd
            def _(pool):
                pool.iota(tab[:, 0:NE], pattern=[[-1, NE]], base=NE, channel_multiplier=0).then_inc(tables, 1)
                pool.iota(tab[:, NE:2 * NE], pattern=[[REG, NE]], base=0, channel_multiplier=0).then_inc(tables, 1)
                pool.iota(tab[:, 2 * NE:2 * NE + ETILES], pattern=[[1, ETILES]], base=0, channel_multiplier=0)\
                    .then_inc(tables, 1)
                pool.iota(dsti[:, :, :], pattern=[[HT, NT], [T, 2]], base=0, channel_multiplier=1).then_inc(tables, 1)
                pool.iota(padi[:, :, :], pattern=[[ST, NE + SPARE], [1, SQ]], base=2 * T, channel_multiplier=SQ)\
                    .then_inc(tables, 1)
                pool.wait_ge(tables, 5)
                pool.tensor_copy(tabf[:, :], tab[:, :]).then_inc(tables, 1)
                pool.tensor_copy(dp[:, :, :, 0], dsti[0:HT, :, :]).then_inc(tables, 1)
                pool.memset(pad[:, :, :, :], 0.0).then_inc(tables, 1)
                pool.wait_ge(tables, 8)

                def set_pad(n, s):
                    pool.tensor_copy(pad[:, s, :, D:D + 1], padi[:, bass.ds(n, 1), :].rearrange("p a q -> p q a"))\
                        .then_inc(pad_set, 1)

                for s in range(PSL):
                    set_pad(s, s)
                with pool.Fori(1, (NE + SPARE) // PSL) as i:
                    for s in range(PSL):
                        pool.wait_ge(pad_out[s], 16 * i)
                        set_pad(PSL * i + s, s)

                with pool.Fori(0, NT // XSL) as i:
                    for s in range(XSL):
                        pool.wait_ge(hb_done, 5 * (XSL * i + s) + 5)
                        pool.sem_inc(sent, 1)
                        for k in range(2):
                            pool.indirect_dma_start(
                                out=slots_d[:, :], out_offset=bass.IndirectOffsetOnAxis(
                                    ap=hbi[:, s, k:k + 1], axis=0),
                                in_=hb[:, s, k, :], in_offset=None).then_inc(hb_out[s], 16)
                for s in range(XSL):
                    pool.wait_ge(hb_out[s], 32 * (NT // XSL))

            @block.sync
            def _(sp):
                def send_pad(n, row):
                    sp.wait_ge(pad_set, n + 1)
                    sp.dma_start(slots_d[bass.ds(row, ST), :].rearrange("(p q) n -> p q n", q=SQ),
                                 pad[:, n % PSL, :, :]).then_inc(pad_out[n % PSL], 16)

                for n in range(SPARE):
                    send_pad(n, NE * REG + n * ST)
                sp.wait_ge(gate_d, 56)
                for n in range(NE):
                    send_pad(SPARE + n, sp.value_load(where[0:1, 2 * ETILES + n:2 * ETILES + n + 1],
                                                      min_val=0, max_val=NE * REG - ST))
                for s in range(PSL):
                    sp.wait_ge(pad_out[s], 16 * (NE + SPARE) // PSL)

            @block.scalar
            def _(act):
                act.wait_ge(gate_d, 7)
                act.activation(st[:, 6, :], st[:, 5, :], ACT.Sqrt).then_inc(gate_a, 1)
                act.wait_ge(gate_d, 26)
                act.activation(st[:, 4, :], st[:, 3, :], ACT.Exp).then_inc(gate_a, 1)

            @block.tensor
            def _(pe):
                pe.wait_ge(gate_d, 25)
                for g in range(2):
                    part = ohb[:, 4 * g:4 * g + 4, :].rearrange("p e t -> p (e t)")
                    pe.matmul(p_kd[0:HT, g, :], trib[0:HT, 0:HT], part, start=True, stop=True)
                    mm = pe.matmul(p_qd[0:HT, g, :], onesb[0:HT, 0:HT], part, start=True, stop=True)
                mm.then_inc(gate_p, 1)

            @block.vector
            def _(dve):
                def steps(n):
                    dve.wait_ge(gate_d, n)

                def tt(out, a, b, op):
                    dve.tensor_tensor(out, a, b, op).then_inc(gate_d, 1)

                def bc(a):
                    return a.unsqueeze(2).to_broadcast([HT, NT, NE])

                tt(st[:, 0, :], bn[:, :, 1], bn[:, :, 4], ALU.add)
                tt(st[:, 1, :], bn[:, :, 1], bn[:, :, 4], ALU.subtract)
                tt(st[:, 2, :], bn[:, :, 2], bn[:, :, 5], ALU.add)
                steps(3)
                dve.tensor_scalar(st[:, 8, :], st[:, 0, :], 0.5, None, ALU.mult).then_inc(gate_d, 1)
                tt(st[:, 3, :], st[:, 1, :], st[:, 1, :], ALU.mult)
                dve.tensor_scalar(st[:, 4, :], st[:, 2, :], 1.0 / D, EPS_LN, ALU.mult, ALU.add).then_inc(gate_d, 1)
                steps(6)
                dve.scalar_tensor_tensor(out=st[:, 5, :], in0=st[:, 3, :], scalar=0.25, in1=st[:, 4, :],
                                         op0=ALU.mult, op1=ALU.add).then_inc(gate_d, 1)
                dve.wait_ge(gate_a, 1)
                dve.reciprocal(st[:, 7, :], st[:, 6, :]).then_inc(gate_d, 1)
                steps(8)
                tt(st[:, 0, :], st[:, 7, :], st[:, 7, :], ALU.mult)
                steps(9)
                tt(st[:, 1, :], st[:, 0, :], st[:, 5, :], ALU.mult)
                steps(10)
                dve.tensor_scalar(st[:, 2, :], st[:, 1, :], -0.5, 1.5, ALU.mult, ALU.add).then_inc(gate_d, 1)
                steps(11)
                tt(st[:, 9, :], st[:, 2, :], st[:, 7, :], ALU.mult)
                steps(12)
                tt(gs[:, :, :], h2v[:, :, D:GC], bc(st[:, 9, :]), ALU.mult)
                steps(13)
                dve.tensor_reduce(st[:, 0, :], gs[:, :, :], AX.X, ALU.max).then_inc(gate_d, 1)
                steps(14)
                tt(oh[:, 0, :, :], gs[:, :, :], bc(st[:, 0, :]), ALU.is_equal)
                dve.wait_ge(tables, 8)
                rev = tabf[0:HT, 0:NE].unsqueeze(1).to_broadcast([HT, NT, NE])
                steps(15)
                tt(tmp[:, :, :], oh[:, 0, :, :], rev, ALU.mult)
                steps(16)
                dve.tensor_reduce(st[:, 1, :], tmp[:, :, :], AX.X, ALU.max).then_inc(gate_d, 1)
                steps(17)
                tt(oh[:, 0, :, :], rev, bc(st[:, 1, :]), ALU.is_equal)
                steps(18)
                dve.scalar_tensor_tensor(out=tmp[:, :, :], in0=oh[:, 0, :, :], scalar=-3e38, in1=gs[:, :, :],
                                         op0=ALU.mult, op1=ALU.add).then_inc(gate_d, 1)
                steps(19)
                dve.tensor_reduce(st[:, 2, :], tmp[:, :, :], AX.X, ALU.max).then_inc(gate_d, 1)
                steps(20)
                tt(oh[:, 1, :, :], tmp[:, :, :], bc(st[:, 2, :]), ALU.is_equal)
                steps(21)
                tt(gs[:, :, :], oh[:, 1, :, :], rev, ALU.mult)
                steps(22)
                dve.tensor_reduce(st[:, 1, :], gs[:, :, :], AX.X, ALU.max).then_inc(gate_d, 1)
                steps(23)
                tt(oh[:, 1, :, :], rev, bc(st[:, 1, :]), ALU.is_equal)
                steps(24)
                tt(ohb[:, :, :].rearrange("p e t -> p t e"), oh[:, 0, :, :], oh[:, 1, :, :], ALU.add)
                tt(st[:, 3, :], st[:, 2, :], st[:, 0, :], ALU.subtract)
                dve.wait_ge(gate_a, 2)
                dve.tensor_scalar(st[:, 5, :], st[:, 4, :], 1.0, None, ALU.add).then_inc(gate_d, 1)
                steps(27)
                dve.reciprocal(dp[:, :, 0, 1], st[:, 5, :]).then_inc(gate_d, 1)
                steps(28)
                tt(dp[:, :, 1, 1], dp[:, :, 0, 1], st[:, 4, :], ALU.mult)
                dve.wait_ge(gate_p, 1)
                total = p_qd[0:HT, :, :].rearrange("p g n -> p (g n)").rearrange("p (e t) -> p e t", e=NE)
                before = p_kd[0:HT, :, :].rearrange("p g n -> p (g n)").rearrange("p (e t) -> p e t", e=NE)
                for e in range(NE):
                    dve.tensor_tensor_scan(run[:, e, :], total[:, e, :], ones[0:HT, 0:NT], 0.0, ALU.add, ALU.mult)\
                       .then_inc(gate_d, 1)
                steps(37)
                tt(rank[:, :, :], run[:, :, :], total, ALU.subtract)
                steps(38)
                tt(rank[:, :, :], rank[:, :, :], before, ALU.add)
                steps(39)
                tt(rank[:, :, :], rank[:, :, :], tabf[0:HT, NE:2 * NE].unsqueeze(2).to_broadcast([HT, NE, NT]), ALU.add)
                steps(40)
                for k in range(2):
                    tt(tmp[:, :, :], oh[:, k, :, :], rank[:, :, :].rearrange("p e t -> p t e"), ALU.mult)
                    steps(41 + 2 * k)
                    dve.tensor_reduce(idx[:, :, k], tmp[:, :, :], AX.X, ALU.add).then_inc(gate_d, 1)
                    steps(42 + 2 * k)
                cnt = run[:, :, NT - 1]
                c = cx[0:HT]
                big = float(1 << 23)
                dve.tensor_scalar(c[:, 0, :], cnt, 1.0 / ST, (ST - 1) / (2.0 * ST), ALU.mult, ALU.add).then_inc(gate_d, 1)
                steps(45)
                dve.tensor_scalar(c[:, 1, :], c[:, 0, :], big, None, ALU.add).then_inc(gate_d, 1)
                steps(46)
                dve.tensor_scalar(c[:, 2, :], c[:, 1, :], big, None, ALU.subtract).then_inc(gate_d, 1)
                steps(47)
                dve.tensor_tensor_scan(c[:, 3, :], c[:, 2, :], ones[0:HT, 0:NE], 0.0, ALU.add, ALU.mult).then_inc(gate_d, 1)
                dve.tensor_scalar(c[:, 4, :], c[:, 2, :], -float(ST), float(REG), ALU.mult, ALU.add).then_inc(gate_d, 1)
                steps(49)
                done = tl[0:HT, 0]
                number = tabf[0:HT, 2 * NE:2 * NE + ETILES]
                tt(done, c[:, 3, :].unsqueeze(1).to_broadcast([HT, ETILES, NE]),
                   number.unsqueeze(2).to_broadcast([HT, ETILES, NE]), ALU.is_le)
                steps(50)
                tt(tl[0:HT, 1], done, c[:, 4, :].unsqueeze(1).to_broadcast([HT, ETILES, NE]), ALU.mult)
                dve.tensor_reduce(tj[0:HT, 0], done, AX.X, ALU.add).then_inc(gate_d, 1)
                steps(52)
                dve.tensor_reduce(tj[0:HT, 1], tl[0:HT, 1], AX.X, ALU.add).then_inc(gate_d, 1)
                dve.tensor_scalar(where[:, ETILES:2 * ETILES], tj[0:1, 0], NE - 1.0, None, ALU.min).then_inc(gate_d, 1)
                steps(54)
                dve.scalar_tensor_tensor(out=where[:, 0:ETILES], in0=number[0:1], scalar=float(ST), in1=tj[0:1, 1],
                                         op0=ALU.mult, op1=ALU.add).then_inc(gate_d, 1)
                tt(where[:, 2 * ETILES:], cnt[0:1], tabf[0:1, NE:2 * NE], ALU.add)
                steps(56)

                def token_rows(n, s):
                    dve.tensor_copy(hbi[:, s, :], idx[:, bass.ds(n, 1), :].rearrange("p a k -> p (a k)"))\
                       .then_inc(hb_done, 1)
                    for k in range(2):
                        dve.tensor_scalar(hb[:, s, k, 0:D], h2v[:, bass.ds(n, 1), 0:D].rearrange("p a n -> p (a n)"),
                                          st[:, 8, bass.ds(n, 1)], st[:, 9, bass.ds(n, 1)], ALU.subtract, ALU.mult)\
                           .then_inc(hb_done, 1)
                        dve.tensor_copy(hb[:, s, k, D:ROW], dp[:, bass.ds(n, 1), k, :].rearrange("p a n -> p (a n)"))\
                           .then_inc(hb_done, 1)

                for s in range(XSL):
                    token_rows(s, s)
                with dve.Fori(1, NT // XSL) as i:
                    for s in range(XSL):
                        dve.wait_ge(hb_out[s], 32 * i)
                        token_rows(XSL * i + s, s)

        with nc.Block() as block:

            @block.sync
            def _(sp):
                def place(n):
                    return (sp.value_load(where[0:1, bass.ds(n, 1)], min_val=0, max_val=XROWS - ST),
                            sp.value_load(where[0:1, bass.ds(n + ETILES, 1)], min_val=0, max_val=NE - 1))

                def load_x(row, s):
                    sp.dma_start(xin[:, s, :, :], slots_d[bass.ds(row, ST), :].rearrange("(p q) n -> p q n", q=SQ))\
                      .then_inc(x_ld[s], 16)

                def load_w(e, s):
                    sp.dma_start(w1t[:, s, :, :], w1[bass.ds(e, 1)].rearrange("a (c p) n -> (a p) c n", p=NPART))\
                      .then_inc(w_ld[s], 16)
                    sp.dma_start(b1t[:, s, :], b1[bass.ds(e, 1)].rearrange("a (m p) -> (a p) m", p=128),
                                 allow_slow_non_contiguous=True).then_inc(w_ld[s], 16)
                    sp.dma_start(w2t[:, s, :, :], w2[bass.ds(e, 1)].rearrange("a (m p) n -> (a p) m n", p=128))\
                      .then_inc(w_ld[s], 16)
                    sp.dma_start(b2t[:, s, :], b2[bass.ds(e, 1)].to_broadcast([128, D]))\
                      .then_inc(w_ld[s], 16)

                for s in range(2):
                    row, e = place(s)
                    load_x(row, s)
                    load_w(e, s)
                with sp.Fori(1, ETILES // 2) as i:
                    for s in range(2):
                        row, e = place(2 * i + s)
                        sp.wait_ge(ypr_done, 2 * (2 * i + s - 1))
                        sp.sem_inc(begun, 1)
                        load_x(row, s)
                        sp.wait_ge(ys_b, 2 * i + s - 1)
                        sp.sem_inc(begun, 1)
                        load_w(e, s)

            @block.tensor
            def _(pe):
                def turn(n, i, s, first=False):
                    pe.wait_ge(x_ld[s], 16 * i + 16)
                    if not first:
                        pe.wait_ge(xt_done, 2 * n)
                    for c in range(2):
                        for q in range(SQ):
                            mm = pe.transpose(p_kd[0:NPART, c, 128 * q:128 * q + 128],
                                              xin[:, s, q, NPART * c:NPART * c + NPART], ident[:, :])
                    mm.then_inc(xt_ps, 1)

                def hidden(n, i, s, first=False):
                    pe.wait_ge(w_ld[s], 64 * i + 64)
                    pe.wait_ge(xt_done, 2 * n + 2)
                    for m in range(3):
                        if not first:
                            pe.wait_ge(hid_done, 3 * n + m - 2)
                        for c in range(2):
                            mm = pe.matmul((p_qk, p_m, p_qd[:, 0, :])[m][:, :], w1t[:, s, c, 128 * m:128 * m + 128],
                                           xtr[:, s, c, :], start=(c == 0), stop=(c == 1))
                        mm.then_inc(hid_ps, 1)

                def output(n, s, first=False):
                    pe.wait_ge(hid_done, 3 * n + 3)
                    if not first:
                        pe.wait_ge(ys_b, n)
                    for q in range(SQ):
                        for m in range(3):
                            mm = pe.matmul(p_qt[:, q // 2, D * (q % 2):D * (q % 2) + D],
                                           hid[:, s, m, 128 * q:128 * q + 128], w2t[:, s, m, :],
                                           start=(m == 0), stop=(m == 2))
                    mm.then_inc(ys_ps, 1)

                turn(0, 0, 0, first=True)
                hidden(0, 0, 0, first=True)
                turn(1, 0, 1)
                output(0, 0, first=True)
                with pe.Fori(0, ETILES // 2 - 1) as i:
                    for s in range(2):
                        n = 2 * i + s + 1
                        hidden(n, i + s, 1 - s)
                        turn(n + 1, i + 1, s)
                        output(n, 1 - s)
                hidden(ETILES - 1, ETILES // 2 - 1, 1)
                output(ETILES - 1, 1)

            @block.scalar
            def _(act):
                def tile(n, s, first=False):
                    if not first:
                        act.wait_ge(ys_ps, n - 1)
                    for m in range(3):
                        act.wait_ge(hid_ps, 3 * n + m + 1)
                        act.activation(hid[:, s, m, :], (p_qk, p_m, p_qd[:, 0, :])[m][:, :], ACT.Gelu,
                                       bias=b1t[:, s, m:m + 1]).then_inc(hid_done, 1)

                for s in range(2):
                    tile(s, s, first=True)
                with act.Fori(1, ETILES // 2) as i:
                    for s in range(2):
                        tile(2 * i + s, s)

            @block.vector
            def _(dve):
                def turned(n, i, s, first=False):
                    dve.wait_ge(xt_ps, n + 1)
                    if not first:
                        dve.wait_ge(hid_ps, 3 * n - 3)
                    for c in range(2):
                        dve.tensor_copy(xtr[:, s, c, :], p_kd[0:NPART, c, :]).then_inc(xt_done, 1)
                    if not first:
                        dve.wait_ge(ys_done, n - 1)
                        dve.wait_ge(ys_out[s], 64 * i)
                    dve.tensor_copy(ypr[:, s, :], xin[:, s, :, D + 1]).then_inc(ypr_done, 1)
                    dve.tensor_copy(ydst[:, s, :], xin[:, s, :, D]).then_inc(ypr_done, 1)

                def results(n, i, s, first=False):
                    dve.wait_ge(ys_ps, n + 1)
                    if not first:
                        dve.wait_ge(ys_out[s], 64 * i)
                    y = ys[:, s, :, :]
                    dve.tensor_tensor(y.rearrange("p (g q) n -> p g q n", g=2),
                                      p_qt[:, :, 0:2 * D].rearrange("p g (q n) -> p g q n", q=2),
                                      b2t[:, s, :].unsqueeze(1).unsqueeze(1).to_broadcast([128, 2, 2, D]), ALU.add)\
                       .then_inc(ys_b, 1)
                    dve.wait_ge(ys_b, n + 1)
                    dve.wait_ge(ypr_done, 2 * n + 2)
                    dve.tensor_tensor(y, y, ypr[:, s, :].unsqueeze(2).to_broadcast([128, SQ, D]), ALU.mult)\
                       .then_inc(ys_done, 1)

                turned(0, 0, 0, first=True)
                turned(1, 0, 1, first=True)
                results(0, 0, 0, first=True)
                turned(2, 1, 0)
                results(1, 0, 1, first=True)
                with dve.Fori(1, ETILES // 2 - 1) as i:
                    for s in range(2):
                        turned(2 * i + s + 1, i + s, 1 - s)
                        results(2 * i + s, i, s)
                turned(ETILES - 1, ETILES // 2 - 1, 1)
                results(ETILES - 2, ETILES // 2 - 1, 0)
                results(ETILES - 1, ETILES // 2 - 1, 1)

            @block.gpsimd
            def _(pool):
                with pool.Fori(0, ETILES // 2) as i:
                    for s in range(2):
                        pool.wait_ge(ys_done, 2 * i + s + 1)
                        pool.sem_inc(sent, 1)
                        for q in range(SQ):
                            pool.indirect_dma_start(
                                out=y_d[:, :], out_offset=bass.IndirectOffsetOnAxis(ap=ydst[:, s, q:q + 1], axis=0),
                                in_=ys[:, s, q, :], in_offset=None).then_inc(ys_out[s], 16)
                for s in range(2):
                    pool.wait_ge(ys_out[s], 64 * (ETILES // 2))

        y_v = y_d[0:2 * T, :].rearrange("(k t p) n -> t k p n", k=2, p=HT)
        out_v = out.rearrange("b (h p) n -> (b h) p n", p=HT)
        with nc.Block() as block:

            @block.sync
            def _(sp):
                def load(g, s):
                    for t in range(GG):
                        sp.dma_start(yin[:, s, t, :, :],
                                     y_v[bass.ds(GG * g + t, 1)].rearrange("a k p n -> (a p) k n"))\
                          .then_inc(yin_ld[s], 16)

                for s in range(YSL):
                    load(s, s)
                with sp.Fori(1, NT // GG // YSL) as i:
                    for s in range(YSL):
                        sp.wait_ge(sum1, YSL * i + s - YSL + 1)
                        load(YSL * i + s, s)

            @block.vector
            def _(dve):
                with dve.Fori(0, NT // GG // YSL) as i:
                    for s in range(YSL):
                        g = YSL * i + s
                        dve.wait_ge(yin_ld[s], 16 * GG * (i + 1))
                        rows = h2v[:, bass.ds(GG * g, GG), 0:D]
                        dve.tensor_tensor(yin[:, s, :, 0, :], yin[:, s, :, 0, :], yin[:, s, :, 1, :], ALU.add)\
                           .then_inc(sum0, 1)
                        dve.wait_ge(sum0, g + 1)
                        dve.tensor_tensor(rows, rows, yin[:, s, :, 0, :], ALU.add).then_inc(sum1, 1)

            @block.scalar
            def _(act):
                with act.Fori(0, NT // GG) as g:
                    act.wait_ge(sum1, g + 1)
                    act.dma_start(out_v[bass.ds(GG * g, GG)].rearrange("t p n -> p t n"),
                                  h2v[:, bass.ds(GG * g, GG), 0:D]).then_inc(o_out, 16)
                act.wait_ge(o_out, 16 * (NT // GG))


_INS = ['x', 'L0_tok_channel_weights', 'L0_attn_W_qkv', 'L0_attn_W_proj', 'L0_attn_b_proj', 'L0_attn_proj_mat',
        'L0_ffn_Wg', 'L0_ffn_W1', 'L0_ffn_b1', 'L0_ffn_W2', 'L0_ffn_b2']
_OUTS = [((64, 196, 192), 'float32')]


def kernel(**inputs):
    import numpy as _np
    import concourse.bacc as _bacc
    from concourse import mybir as _mybir
    from concourse.bass_utils import run_bass_kernel_spmd as _run

    nc = _bacc.Bacc("TRN2", target_bir_lowering=False, num_devices=1)
    arrays, args = {}, []
    for name in _INS:
        a = _np.ascontiguousarray(inputs[name])
        arrays[f"in_{name}_dram"] = a
        args.append(nc.dram_tensor(f"in_{name}_dram", a.shape, _mybir.dt.from_np(a.dtype), kind="ExternalInput").ap())
    for i, (shape, dtype) in enumerate(_OUTS):
        dt = _mybir.dt.from_np(_np.dtype(dtype))
        args.append(nc.dram_tensor(f"out_{i}_dram", shape, dt, kind="ExternalOutput").ap())
    vit_block(nc, *args)
    r = _run(nc, [arrays], core_ids=[0])
    got = tuple(r.results[0][f"out_{i}_dram"] for i in range(len(_OUTS)))
    return got[0]
```

```python
from contextlib import ExitStack

import concourse.bass as bass
from concourse import mybir

ALU = mybir.AluOpType
ACT = mybir.ActivationFunctionType
AX = mybir.AxisListType
F32 = mybir.dt.float32
BF16 = mybir.dt.bfloat16
I32 = mybir.dt.int32
U32 = mybir.dt.uint32
F32R = mybir.dt.float32r

B, C, IMG, PATCH = 64, 12, 224, 16
NP = IMG // PATCH
TOK = NP * NP
HT = TOK // 2
NT = 2 * B
T = B * TOK
D = 192
NH, HD, M = 12, 16, 44
HM = NH * M
HALF = HM // 2
PAIRS = NH // 2
PM = 2 * M
UC = C + 1
UW = 32
WIN = 8 * UC
STEP = WIN + 2 * UC
EPS_F = 1e-4
EPS_LN = 1e-5
K6 = 6 * C
NPART = 6 * HD
NE, HID = 8, 384
GC = D + NE
ROW = D + 2
ST = 512
SQ = ST // 128
ETILES = (2 * T + NE * (ST - 1)) // ST
REG = T + ST
SPARE = 8
XROWS = NE * REG + SPARE * ST
YROWS = 2 * T + (NE + SPARE) * ST
ROWS = B * C * NP
STRIP = PATCH * IMG
XT = ROWS // 128
XS = 4
CDQ, CDK = 2 * D, 2 * D + HM
WC = 2 * D + 2 * HM
VH = 6 * C
PL = 96
KCH = 112
Q = 4
QT = NT // Q
QK = T // KCH // Q
assert B == 16 * Q and XT == 4 * XS * (Q + 1) + XS
ROUNDS = XT // XS
WORK = 10350
XSL = 4
PSL = 4
YSL = 4
GG = 4


def vit_block(nc, x, cw, w_qkv, w_proj, b_proj, proj, wg, w1, b1, w2, b2, out):
    with ExitStack() as ctx:
        def sb(name, shape, dt=F32):
            return ctx.enter_context(nc.sbuf_tensor(name, shape, dt))

        def sem(name):
            return ctx.enter_context(nc.semaphore(name))

        def sems(name, n):
            return [sem(f"{name}{i}") for i in range(n)]

        pooled_d = nc.dram_tensor("pooled_d", [B, C, TOK], F32).ap()
        slots_d = nc.dram_tensor("slots_d", [XROWS, ROW], F32).ap()
        y_d = nc.dram_tensor("y_d", [YROWS, D], F32).ap()

        h2 = sb("h2", [128, NT * GC])
        xt = h2[:, 0:XS * STRIP].rearrange("p (s n) -> p s n", s=XS)
        h2v = h2[0:HT, :].rearrange("p (t n) -> p t n", t=NT)
        us32 = sb("us32", [128, T // 2])
        us = us32[:, :].bitcast(BF16)
        work = sb("work", [128, WORK])

        def carve(at, rows, shape, dt=F32, of=work):
            size = 1
            for n in shape:
                size *= n
            words = (size + 1) // 2 if dt == BF16 else size
            part = of[0:rows, at:at + words]
            if dt != F32:
                part = part.bitcast(dt)
            names = [f"n{i}" for i in range(len(shape))]
            if len(shape) > 1:
                part = part.rearrange(f"p ({' '.join(names)}) -> p {' '.join(names)}",
                                      **dict(zip(names[1:], shape[1:])))
            return part, at + words

        strips = sb("strips", [128, XS, NP])
        ident = sb("ident", [128, 128])
        identb = sb("identb", [128, 128], BF16)
        negib = sb("negib", [128, 128], BF16)
        ones = sb("ones", [128, 128])
        onesb = sb("onesb", [128, 128], BF16)
        trib = sb("trib", [128, 128], BF16)
        epsc = sb("epsc", [128, 1])
        ind3 = sb("ind3", [128, HM], BF16)
        umask = sb("umask", [PM, 3, 2, UC])
        vmask = sb("vmask", [NPART, 6])
        wvp = sb("wvp", [128, 2, GC])
        gram = sb("gram", [C, C])
        w72 = sb("w72", [128, WC], BF16)
        uu, end = carve(0, HT, [NT, K6], BF16)
        pcr, end = carve(end, C, [T // Q])
        var1, end = carve(end, HT, [6, NT])
        pt, end = carve(XS * STRIP, HT, [NT, C], of=h2)
        gp, end = carve(end, HT, [NT, C], of=h2)
        wall, end = carve(end, C, [WC], of=h2)
        wparts, end = carve(end, C, [3, WC], BF16, of=h2)
        wqkv_s, end = carve(end, NPART, [2, 3 * D], of=h2)
        bd, end = carve(end, NPART, [HALF], of=h2)
        wpt, end = carve(end, NPART, [2, D], of=h2)
        bv, end = carve(end, NPART, [2, 6, C], of=h2)
        cw13t, end = carve(end, NPART, [2, C + 1], of=h2)
        cwct, end = carve(end, NPART, [2, C], of=h2)
        w12t, end = carve(end, NPART, [6, C], of=h2)
        wg_s, end = carve(end, NPART, [2, NE], of=h2)
        wgc, end = carve(end, NPART, [2, NE], of=h2)
        cwm, end = carve(end, C, [2], of=h2)
        cw13, end = carve(end, C + 1, [D], of=h2)
        cwc, end = carve(end, C, [D], of=h2)
        wproj_s, end = carve(end, NPART, [2, GC], of=h2)
        km, end = carve(end, KCH, [T // KCH], of=h2)
        cwg, end = carve(end, C + 1, [GC], of=h2)
        assert end <= NT * GC
        kmx = sb("kmx", [128, 3])
        ek, end = carve(0, HT, [2, 2, HM])
        ut = sb("ut", [HT, NT, C])
        u1s = sb("u1s", [HT, 2, 2, 2, UW])
        kuw = sb("kuw", [128, 2, 3 * STEP + 3 * WIN + 2 * UC])
        dk, end = carve(end, HT, [2, 2, NH])
        kut, end = carve(end, 2 * UW, [HALF])
        sq, end = carve(end, HT, [2, 2 * D])
        ss = sb("ss", [HT, 2, 2, 2 * NH])
        qm = sb("qm", [HT, 2, 2, NH])
        shf = sb("shf", [HT, 3, 2, NH])
        s3 = sb("s3", [HT, 2, 3 * NH], BF16)
        sht = sb("sht", [128, TOK], BF16)
        eqt, end = carve(end, 128, [2, PAIRS, TOK])
        rd = sb("rd", [HT, 2, NH])
        at, end = carve(end, HT, [2, 2, NH * C])
        ats = sb("ats", [128, 2, 2, TOK])
        bn = sb("bn", [HT, NT, 6])
        gs, end = carve(end, HT, [QT, NE])
        oh, end = carve(end, HT, [2, QT, NE])
        tmp, end = carve(end, HT, [QT, NE])
        ohb, end = carve(end, HT, [NE, QT], BF16)
        run, end = carve(end, HT, [NE, QT])
        rank, end = carve(end, HT, [NE, QT])
        st, end = carve(end, HT, [10, QT])
        dp, end = carve(end, HT, [QT, 2, 2])
        idx, end = carve(end, HT, [QT, 2])
        hb, end = carve(end, HT, [XSL, 2, ROW])
        hbi, end = carve(end, HT, [XSL, 2], U32)
        dsti, end = carve(end, 128, [NT, 2], I32)
        padi, end = carve(end, 128, [NE + SPARE, SQ], I32)
        tab, end = carve(end, 128, [2 * NE + ETILES], I32)
        tabf, end = carve(end, 128, [2 * NE + ETILES])
        seen, end = carve(end, HT, [NE])
        assert end <= WORK
        pad, end = carve(0, 128, [PSL, SQ, ROW], of=us32)
        cx, end = carve(end, 128, [8, NE], of=us32)
        tl, end = carve(end, 128, [2, ETILES, NE], of=us32)
        tj, end = carve(end, 128, [2, ETILES], of=us32)
        assert end <= T // 2
        where = sb("where", [1, 2 * ETILES + NE], I32)
        xtr = sb("xtr", [NPART, 2, 2, ST], F32R)
        w1r = sb("w1r", [NPART, 2, 2 * HID], F32R)
        w1t, end = carve(0, NPART, [2, 2 * HID], of=us32)
        w2t, end = carve(end, 128, [2, 3, D], of=us32)
        assert end <= T // 2
        xin, end = carve(0, 128, [2, SQ, ROW])
        b1t, end = carve(end, 128, [2, 3])
        b2t, end = carve(end, 128, [2, D])
        hid, end = carve(end, 128, [3, ST])
        ys, end = carve(end, 128, [2, SQ, D])
        ypr, end = carve(end, 128, [2, SQ, 2])
        ydst, end = carve(end, 128, [2, SQ], U32)
        assert end <= WORK
        yin, end = carve(0, HT, [YSL, GG, 2, D])
        assert end <= WORK

        p_kd = ctx.enter_context(nc.psum_tensor("p_kd", [128, 2, 512], F32))
        p_qd = ctx.enter_context(nc.psum_tensor("p_qd", [128, 2, 512], F32))
        p_qk = ctx.enter_context(nc.psum_tensor("p_qk", [128, 512], F32))
        p_m = ctx.enter_context(nc.psum_tensor("p_m", [128, 512], F32))
        p_qt = ctx.enter_context(nc.psum_tensor("p_qt", [128, 2, 512], F32))

        x_in = sems("x_in", XS)
        pooled = sem("pooled")
        strip_out = sems("strip_out", XS)
        w_in = sem("w_in")
        bd_in = sem("bd_in")
        pads = sem("pads")
        eqt_set = sem("eqt_set")
        cst = sem("cst")
        dz = sem("dz")
        bdz = sem("bdz")
        setup_d = sem("setup_d")
        setup_p = sem("setup_p")
        setup_a = sem("setup_a")
        w72_in = sem("w72_in")
        cwg_in = sem("cwg_in")
        bvm = sem("bvm")
        pc_in = sem("pc_in")
        pc_last = sem("pc_last")
        pt_ps = sem("pt_ps")
        pt_cp = sem("pt_cp")
        ln1 = sem("ln1")
        ln1a = sem("ln1a")
        us_ps = sem("us_ps")
        us_cp = sem("us_cp")
        km_ps = sem("km_ps")
        km_cp = sem("km_cp")
        km_fin = sem("km_fin")
        km_all = sem("km_all")
        stab = sem("stab")
        qk_ready = sem("qk_ready")
        kd_ready = sem("kd_ready")
        qd_ready = sem("qd_ready")
        sq_done = sem("sq_done")
        ek_done = sem("ek_done")
        dk_done = sem("dk_done")
        ss_done = sem("ss_done")
        qm_done = sem("qm_done")
        u1_done = sem("u1_done")
        k1_done = sem("k1_done")
        sh_step = sem("sh_step")
        sh_ps = sem("sh_ps")
        sht_done = sem("sht_done")
        qt_ps = sem("qt_ps")
        eq_done = sem("eq_done")
        kut_ps = sem("kut_ps")
        kut_done = sem("kut_done")
        ku_ps = sem("ku_ps")
        kuw_done = sem("kuw_done")
        eqe_done = sem("eqe_done")
        att_ps = sem("att_ps")
        rd_done = sem("rd_done")
        at_done = sem("at_done")
        ats_done = sem("ats_done")
        g_ps = sem("g_ps")
        h2_done = sem("h2_done")
        bn_done = sem("bn_done")
        pl_in = sems("pl_in", 2)
        sent = sem("sent")
        tables = sem("tables")
        gate_d = sem("gate_d")
        gate_a = sem("gate_a")
        gate_p = sem("gate_p")
        pad_set = sem("pad_set")
        pad_out = sems("pad_out", PSL)
        hb_done = sem("hb_done")
        hb_out = sems("hb_out", XSL)
        begun = sem("begun")
        x_ld = sems("x_ld", 2)
        w1_ld = sems("w1_ld", 2)
        w1_hi = sem("w1_hi")
        w1_lo = sem("w1_lo")
        w2_ld = sems("w2_ld", 2)
        xt_ps = sem("xt_ps")
        xt_hi = sem("xt_hi")
        xt_done = sem("xt_done")
        hid_ps = sem("hid_ps")
        hid_done = sem("hid_done")
        ys_ps = sem("ys_ps")
        ys_b = sem("ys_b")
        ypr_done = sem("ypr_done")
        ydst_done = sem("ydst_done")
        ys_done = sem("ys_done")
        ys_out = sems("ys_out", 2)
        yin_ld = sems("yin_ld", YSL)
        sum0 = sem("sum0")
        sum1 = sem("sum1")
        o_out = sem("o_out")

        GSTEPS = 46

        def gate(dve, q):
            o = GSTEPS * q

            def steps(n):
                dve.wait_ge(gate_d, o + n)

            def tt(out, a, b, op):
                dve.tensor_tensor(out, a, b, op).then_inc(gate_d, 1)

            def bc(a):
                return a.unsqueeze(2).to_broadcast([HT, QT, NE])

            tt(st[:, 0, :], bn[:, QT * q:QT * q + QT, 1], bn[:, QT * q:QT * q + QT, 4], ALU.add)
            tt(st[:, 1, :], bn[:, QT * q:QT * q + QT, 1], bn[:, QT * q:QT * q + QT, 4], ALU.subtract)
            tt(st[:, 2, :], bn[:, QT * q:QT * q + QT, 2], bn[:, QT * q:QT * q + QT, 5], ALU.add)
            steps(3)
            dve.tensor_scalar(st[:, 8, :], st[:, 0, :], 0.5, None, ALU.mult).then_inc(gate_d, 1)
            tt(st[:, 3, :], st[:, 1, :], st[:, 1, :], ALU.mult)
            dve.tensor_scalar(st[:, 4, :], st[:, 2, :], 1.0 / D, EPS_LN, ALU.mult, ALU.add).then_inc(gate_d, 1)
            steps(6)
            dve.scalar_tensor_tensor(out=st[:, 5, :], in0=st[:, 3, :], scalar=0.25, in1=st[:, 4, :],
                                     op0=ALU.mult, op1=ALU.add).then_inc(gate_d, 1)
            dve.wait_ge(gate_a, 2 * q + 1)
            dve.reciprocal(st[:, 7, :], st[:, 6, :]).then_inc(gate_d, 1)
            steps(8)
            tt(st[:, 0, :], st[:, 7, :], st[:, 7, :], ALU.mult)
            steps(9)
            tt(st[:, 1, :], st[:, 0, :], st[:, 5, :], ALU.mult)
            steps(10)
            dve.tensor_scalar(st[:, 2, :], st[:, 1, :], -0.5, 1.5, ALU.mult, ALU.add).then_inc(gate_d, 1)
            steps(11)
            tt(st[:, 9, :], st[:, 2, :], st[:, 7, :], ALU.mult)
            steps(12)
            tt(gs[:, :, :], h2v[:, QT * q:QT * q + QT, D:GC], bc(st[:, 9, :]), ALU.mult)
            steps(13)
            dve.tensor_reduce(st[:, 0, :], gs[:, :, :], AX.X, ALU.max).then_inc(gate_d, 1)
            steps(14)
            tt(oh[:, 0, :, :], gs[:, :, :], bc(st[:, 0, :]), ALU.is_equal)
            dve.wait_ge(tables, 6)
            rev = tabf[0:HT, 0:NE].unsqueeze(1).to_broadcast([HT, QT, NE])
            steps(15)
            tt(tmp[:, :, :], oh[:, 0, :, :], rev, ALU.mult)
            steps(16)
            dve.tensor_reduce(st[:, 1, :], tmp[:, :, :], AX.X, ALU.max).then_inc(gate_d, 1)
            steps(17)
            tt(oh[:, 0, :, :], rev, bc(st[:, 1, :]), ALU.is_equal)
            steps(18)
            dve.scalar_tensor_tensor(out=tmp[:, :, :], in0=oh[:, 0, :, :], scalar=-3e38, in1=gs[:, :, :],
                                     op0=ALU.mult, op1=ALU.add).then_inc(gate_d, 1)
            steps(19)
            dve.tensor_reduce(st[:, 2, :], tmp[:, :, :], AX.X, ALU.max).then_inc(gate_d, 1)
            steps(20)
            tt(oh[:, 1, :, :], tmp[:, :, :], bc(st[:, 2, :]), ALU.is_equal)
            steps(21)
            tt(gs[:, :, :], oh[:, 1, :, :], rev, ALU.mult)
            steps(22)
            dve.tensor_reduce(st[:, 1, :], gs[:, :, :], AX.X, ALU.max).then_inc(gate_d, 1)
            steps(23)
            tt(oh[:, 1, :, :], rev, bc(st[:, 1, :]), ALU.is_equal)
            steps(24)
            tt(ohb[:, :, :].rearrange("p e t -> p t e"), oh[:, 0, :, :], oh[:, 1, :, :], ALU.add)
            tt(st[:, 3, :], st[:, 2, :], st[:, 0, :], ALU.subtract)
            dve.wait_ge(gate_a, 2 * q + 2)
            dve.tensor_scalar(st[:, 5, :], st[:, 4, :], 1.0, None, ALU.add).then_inc(gate_d, 1)
            steps(27)
            dve.reciprocal(dp[:, :, 0, 1], st[:, 5, :]).then_inc(gate_d, 1)
            steps(28)
            tt(dp[:, :, 1, 1], dp[:, :, 0, 1], st[:, 4, :], ALU.mult)
            dve.wait_ge(gate_p, q + 1)
            sums = p_m[0:HT, :].rearrange("p (g e t) -> p g e t", g=2, e=NE)
            before, total = sums[:, 0], sums[:, 1]
            for e in range(NE):
                dve.tensor_tensor_scan(run[:, e, :], total[:, e, :], ones[0:HT, 0:QT], seen[:, e:e + 1],
                                       ALU.add, ALU.mult)\
                   .then_inc(gate_d, 1)
            steps(37)
            tt(rank[:, :, :], run[:, :, :], total, ALU.subtract)
            steps(38)
            tt(rank[:, :, :], rank[:, :, :], before, ALU.add)
            steps(39)
            tt(rank[:, :, :], rank[:, :, :], tabf[0:HT, NE:2 * NE].unsqueeze(2).to_broadcast([HT, NE, QT]), ALU.add)
            steps(40)
            for k in range(2):
                tt(tmp[:, :, :], oh[:, k, :, :], rank[:, :, :].rearrange("p e t -> p t e"), ALU.mult)
                steps(41 + 2 * k)
                dve.tensor_reduce(idx[:, :, k], tmp[:, :, :], AX.X, ALU.add).then_inc(gate_d, 1)
                steps(42 + 2 * k)
            dve.tensor_copy(seen[:, :], run[:, :, QT - 1]).then_inc(gate_d, 1)
            dve.tensor_copy(dp[:, :, :, 0], dsti[0:HT, QT * q:QT * q + QT, :]).then_inc(gate_d, 1)
            steps(GSTEPS)

        def token_rows(dve, n, m, s):
            dve.tensor_copy(hbi[:, s, :], idx[:, bass.ds(m, 1), :].rearrange("p a k -> p (a k)")).then_inc(hb_done, 1)
            for k in range(2):
                dve.tensor_scalar(hb[:, s, k, 0:D], h2v[:, bass.ds(n, 1), 0:D].rearrange("p a n -> p (a n)"),
                                  st[:, 8, bass.ds(m, 1)], st[:, 9, bass.ds(m, 1)], ALU.subtract, ALU.mult)\
                   .then_inc(hb_done, 1)
                dve.tensor_copy(hb[:, s, k, D:ROW], dp[:, bass.ds(m, 1), k, :].rearrange("p a n -> p (a n)"))\
                   .then_inc(hb_done, 1)

        def scatter(pool, n, s):
            pool.wait_ge(hb_done, 5 * n + 5)
            pool.sem_inc(sent, 1)
            for k in range(2):
                pool.indirect_dma_start(out=slots_d[:, :],
                                        out_offset=bass.IndirectOffsetOnAxis(ap=hbi[:, s, k:k + 1], axis=0),
                                        in_=hb[:, s, k, :], in_offset=None).then_inc(hb_out[s], 16)

        def gate_roots(act, q):
            act.wait_ge(gate_d, GSTEPS * q + 7)
            act.activation(st[:, 6, :], st[:, 5, :], ACT.Sqrt).then_inc(gate_a, 1)
            act.wait_ge(gate_d, GSTEPS * q + 26)
            act.activation(st[:, 4, :], st[:, 3, :], ACT.Exp).then_inc(gate_a, 1)

        def gate_counts(pe, q):
            pe.wait_ge(gate_d, GSTEPS * q + 25)
            chosen = ohb[:, :, :].rearrange("p e t -> p (e t)")
            pe.matmul(p_m[0:HT, 0:NE * QT], trib[0:HT, 0:HT], chosen, start=True, stop=True)
            pe.matmul(p_m[0:HT, NE * QT:2 * NE * QT], onesb[0:HT, 0:HT], chosen, start=True, stop=True)\
              .then_inc(gate_p, 1)
            pe.wait_ge(gate_d, GSTEPS * q + 39)

        LAG = B // Q + 2
        x_v = x.rearrange("b c (i k) w -> (b c i) (k w)", k=PATCH).rearrange("(t p) n -> t p n", p=128)
        pooled_v = pooled_d.rearrange("b c (i j) -> (b c i) j", j=NP).rearrange("(t p) j -> t p j", p=128)
        pooled_c = pooled_d.rearrange("b c t -> c b t")

        with nc.Block() as block:

            @block.sync
            def _(sp):
                def load(t, s):
                    sp.dma_start(xt[:, s, :], x_v[bass.ds(t, 1)].rearrange("a p n -> (a p) n"))\
                      .then_inc(x_in[s], 16)

                for s in range(XS):
                    load(s, s)
                with sp.Fori(1, ROUNDS) as i:
                    for s in range(XS):
                        sp.wait_ge(pooled, XS * i + s - XS + 1)
                        load(XS * i + s, s)
                for s in range(XS):
                    sp.wait_ge(strip_out[s], 16 * ROUNDS)

                sp.wait_ge(pt_ps, Q - 1)
                sp.dma_start(pcr[:, :].rearrange("c (b t) -> c b t", b=B // Q), pooled_c[:, B // Q * (Q - 1):, :])\
                  .then_inc(pc_last, 16)

                def load_rows(b, s):
                    sp.dma_start(ats[PL:PL + C, s, 1, :], pooled_d[bass.ds(b, 1)].rearrange("a c t -> (a c) t"))\
                      .then_inc(pl_in[s], 16)

                sp.wait_ge(dz, 6)
                for s in range(2):
                    load_rows(s, s)
                with sp.Fori(1, B // 2) as i:
                    for s in range(2):
                        sp.wait_ge(g_ps, 2 * i + s - 1)
                        load_rows(2 * i + s, s)

            @block.gpsimd
            def _(pool):
                pool.memset(ones[:, :], 1.0).then_inc(cst, 1)
                pool.memset(onesb[:, :], 1.0).then_inc(cst, 1)
                pool.memset(epsc[:, :], EPS_F).then_inc(cst, 1)
                pool.memset(ind3[:, :], 1.0).then_inc(cst, 1)
                pool.memset(umask[:, :, :, :], 1.0).then_inc(cst, 1)
                pool.memset(vmask[:, :], 1.0).then_inc(cst, 1)
                pool.memset(negib[:, :], 0.0).then_inc(cst, 1)
                pool.wait_ge(cst, 7)
                pool.affine_select(out=ident[:, :], in_=ones[:, :], compare_op=ALU.is_equal, fill=0.0,
                                   base=0, pattern=[[-1, 128]], channel_multiplier=1).then_inc(cst, 1)
                pool.affine_select(out=identb[:, :], in_=onesb[:, :], compare_op=ALU.is_equal, fill=0.0,
                                   base=0, pattern=[[-1, 128]], channel_multiplier=1).then_inc(cst, 1)
                pool.affine_select(out=negib[:, :], in_=negib[:, :], compare_op=ALU.not_equal, fill=-1.0,
                                   base=0, pattern=[[-1, 128]], channel_multiplier=1).then_inc(cst, 1)
                pool.affine_select(out=trib[:, :], in_=onesb[:, :], compare_op=ALU.is_gt, fill=0.0,
                                   base=0, pattern=[[1, 128]], channel_multiplier=-1).then_inc(cst, 1)
                for par in range(2):
                    part = umask[:, :, par, :]
                    pool.affine_select(out=part, in_=part, compare_op=ALU.is_gt, fill=0.0,
                                       base=M if par == 0 else 1 - M, pattern=[[0, 3], [0, UC]],
                                       channel_multiplier=-1 if par == 0 else 1).then_inc(cst, 1)
                pool.affine_select(out=vmask[:, :], in_=vmask[:, :], compare_op=ALU.is_ge, fill=0.0,
                                   base=0, pattern=[[-HD, 6]], channel_multiplier=1).then_inc(cst, 1)
                pool.wait_ge(cst, 14)
                pool.affine_select(out=vmask[:, :], in_=vmask[:, :], compare_op=ALU.is_ge, fill=0.0,
                                   base=HD - 1, pattern=[[HD, 6]], channel_multiplier=-1).then_inc(cst, 1)
                pool.affine_select(out=ind3[:, :].rearrange("p (h m) -> p h m", h=NH),
                                   in_=ind3[:, :].rearrange("p (h m) -> p h m", h=NH),
                                   compare_op=ALU.is_equal, fill=2.0, base=0,
                                   pattern=[[-1, NH], [0, M]], channel_multiplier=1).then_inc(cst, 1)
                pool.wait_ge(cst, 16)
                pool.affine_select(out=ind3[:, :].rearrange("p (h m) -> p h m", h=NH),
                                   in_=ind3[:, :].rearrange("p (h m) -> p h m", h=NH),
                                   compare_op=ALU.not_equal, fill=1.0, base=-NH,
                                   pattern=[[-1, NH], [0, M]], channel_multiplier=1).then_inc(cst, 1)
                pool.wait_ge(cst, 17)
                pool.affine_select(out=ind3[:, :].rearrange("p (h m) -> p h m", h=NH),
                                   in_=ind3[:, :].rearrange("p (h m) -> p h m", h=NH),
                                   compare_op=ALU.not_equal, fill=1.0, base=-2 * NH,
                                   pattern=[[-1, NH], [0, M]], channel_multiplier=1).then_inc(cst, 1)
                pool.wait_ge(cst, 18)
                pool.tensor_scalar(ind3[:, :], ind3[:, :], 1.0, None, ALU.is_equal).then_inc(cst, 1)

                pool.iota(tab[:, 0:NE], pattern=[[-1, NE]], base=NE, channel_multiplier=0).then_inc(tables, 1)
                pool.iota(tab[:, NE:2 * NE], pattern=[[REG, NE]], base=0, channel_multiplier=0).then_inc(tables, 1)
                pool.iota(tab[:, 2 * NE:2 * NE + ETILES], pattern=[[1, ETILES]], base=0, channel_multiplier=0)\
                    .then_inc(tables, 1)
                pool.iota(dsti[:, :, :], pattern=[[HT, NT], [T, 2]], base=0, channel_multiplier=1).then_inc(tables, 1)
                pool.iota(padi[:, :, :], pattern=[[ST, NE + SPARE], [1, SQ]], base=2 * T, channel_multiplier=SQ)\
                    .then_inc(tables, 1)
                pool.wait_ge(tables, 5)
                pool.tensor_copy(tabf[:, :], tab[:, :]).then_inc(tables, 1)

                for q in range(Q - 1):
                    for s in range(XS):
                        pool.wait_ge(strip_out[s], 16 * (5 * q + 6))
                    if q > 0:
                        pool.wait_ge(pt_ps, q)
                    pool.dma_start(pcr[:, :].rearrange("c (b t) -> c b t", b=B // Q),
                                   pooled_c[:, B // Q * q:B // Q * (q + 1), :]).then_inc(pc_in, 16)

                pool.wait_ge(us_cp, NT // GG)
                pool.wait_ge(tables, 6)
                pool.memset(eqt[64:128, :, :, :], 0.0).then_inc(eqt_set, 1)
                pool.wait_ge(eqt_set, 1)
                pool.wait_ge(km_fin, 1)
                pool.partition_all_reduce(kmx[0:KCH, 1:2], kmx[0:KCH, 0:1], KCH, bass.bass_isa.ReduceOp.max)\
                    .then_inc(km_all, 1)

                def key_features(b, s, t):
                    pool.wait_ge(dk_done, 2 * b + t + 1)
                    e = ek[:, s, t, :].rearrange("p (h m) -> p h m", m=M)
                    pool.tensor_tensor(e, e, dk[:, s, t, :].unsqueeze(2).to_broadcast([HT, NH, M]), ALU.mult)\
                        .then_inc(k1_done, 1)

                for t in range(2):
                    key_features(0, 0, t)

                def image(b, s, more=True, rows=True):
                    for t in range(2):
                        if more:
                            key_features(b + 1, 1 - s, t)
                        if rows:
                            scatter(pool, 2 * (b - LAG) + t, 2 * s + t)

                with pool.Fori(0, LAG // 2) as i:
                    image(2 * i, 0, rows=False)
                    image(2 * i + 1, 1, rows=False)
                with pool.Fori(LAG // 2, B // 2 - 1) as i:
                    image(2 * i, 0)
                    image(2 * i + 1, 1)
                image(B - 2, 0)
                image(B - 1, 1, more=False)
                for n in range(2 * (B - LAG), QT * (Q - 1)):
                    scatter(pool, n, n % XSL)

            @block.scalar
            def _(act):
                def first_stores():
                    for s in range(XS):
                        act.wait_ge(pooled, s + 1)
                        act.dma_start(pooled_v[s], strips[:, s, :]).then_inc(strip_out[s], 16)

                act.dma_start(cw13[0:C, :], cw).then_inc(w_in, 16)
                act.dma_start(cw13[C:C + 1, :], b_proj.rearrange("(a n) -> a n", a=1)).then_inc(w_in, 16)
                act.dma_start(wqkv_s[:, :, :], w_qkv.rearrange("(c p) n -> p c n", p=NPART)).then_inc(w_in, 16)
                act.dma_start(wproj_s[:, :, 0:D], w_proj.rearrange("(c p) n -> p c n", p=NPART)).then_inc(w_in, 16)
                act.dma_start(wg_s[:, :, :], wg.rearrange("(c p) n -> p c n", p=NPART)).then_inc(w_in, 16)
                act.wait_ge(bdz, 1)
                for h in range(6):
                    act.dma_start(bd[HD * h:HD * h + HD, M * h:M * h + M], proj.rearrange("m d -> d m"),
                                  allow_slow_non_contiguous=True)\
                       .then_inc(bd_in, 16)

                first_stores()
                act.wait_ge(setup_p, 1)
                act.copy(cwct[:, :, :], p_m[0:NPART, 0:2 * C].rearrange("p (c n) -> p c n", c=2)).then_inc(setup_a, 1)
                act.copy(cw13t[:, :, :], p_m[0:NPART, 32:32 + 2 * (C + 1)].rearrange("p (c n) -> p c n", c=2))\
                   .then_inc(setup_a, 1)
                act.copy(wpt[:, :, :], p_m[0:NPART, 64:64 + 2 * D].rearrange("p (c n) -> p c n", c=2)).then_inc(setup_a, 1)
                act.wait_ge(setup_p, 2)
                act.copy(wall[:, 0:2 * D], p_kd[0:C, 0, 0:2 * D]).then_inc(setup_a, 1)
                act.copy(w12t[:, :, :], p_qd[0:NPART, 0, 0:6 * C].rearrange("p (c n) -> p c n", c=6)).then_inc(setup_a, 1)
                act.mul(gram[:, :], p_qd[0:C, 1, 0:C], 1.0 / D).then_inc(setup_a, 1)
                act.copy(cwg[:, D:GC], p_qk[0:C + 1, 0:NE]).then_inc(setup_a, 1)
                for g in range(2):
                    act.copy(wproj_s[:, g, D:GC], p_qk[0:NPART, 16 + 16 * g:16 + 16 * g + NE]).then_inc(setup_a, 1)
                act.wait_ge(w_in, 80)
                act.copy(cwg[:, 0:D], cw13[:, :]).then_inc(setup_a, 1)
                act.wait_ge(setup_a, 10)
                act.wait_ge(dz, 6)
                act.dma_start(wvp[PL:PL + C + 1, 1, :], cwg[:, :]).then_inc(cwg_in, 16)
                act.wait_ge(setup_p, 3)
                for g in range(4):
                    src = (p_kd, p_kd, p_qt, p_qt)[g]
                    act.mul(wall[:, CDQ + HALF * g:CDQ + HALF * g + HALF], src[0:C, g % 2, 0:HALF], 0.5)\
                       .then_inc(setup_a, 1)
                for g in range(2):
                    act.copy(wvp[0:VH, g, :], p_m[0:VH, GC * g:GC * g + GC]).then_inc(setup_a, 1)
                act.wait_ge(setup_d, 7)
                for r, part in enumerate((0, 1, 2, 0, 1, 0)):
                    if r == 0:
                        act.wait_ge(pads, 2)
                    act.dma_start(w72[C * r:C * r + C, :], wparts[:, part, :]).then_inc(w72_in, 16)

                def store(i):
                    for s in range(XS):
                        act.wait_ge(pooled, XS * i + s + 1)
                        act.dma_start(pooled_v[bass.ds(XS * i + s, 1)].rearrange("a p j -> (a p) j"),
                                      strips[:, s, :]).then_inc(strip_out[s], 16)

                def token_rows(q):
                    act.wait_ge(pt_ps, q + 1)
                    act.copy(pt[:, bass.ds(QT * q, QT), :], p_m[0:HT, 0:QT * C].rearrange("p (t c) -> p t c", t=QT))\
                       .then_inc(pt_cp, 1)
                    act.copy(gp[:, bass.ds(QT * q, QT), :], p_qk[0:HT, 0:QT * C].rearrange("p (t c) -> p t c", t=QT))\
                       .then_inc(pt_cp, 1)

                def split(q):
                    t = bass.ds(QT * q, QT)
                    act.wait_ge(ln1, 13 * q + 3)
                    act.activation(var1[:, 1, t], var1[:, 0, t], ACT.Sqrt).then_inc(ln1a, 1)
                    act.wait_ge(ln1, 13 * q + 10)
                    act.copy(uu[:, t, C:2 * C], uu[:, t, 0:C]).then_inc(ln1a, 1)
                    act.copy(uu[:, t, 2 * C:3 * C], uu[:, t, 0:C]).then_inc(ln1a, 1)
                    act.wait_ge(ln1, 13 * q + 12)
                    act.copy(uu[:, t, 4 * C:5 * C], uu[:, t, 3 * C:4 * C]).then_inc(ln1a, 1)
                    for g in range(QT // GG):
                        n = QT // GG * q + g
                        act.wait_ge(us_ps, n + 1)
                        act.copy(us[0:K6, bass.ds(n * GG * HT, GG * HT)], p_kd[0:K6, g % 2, 0:GG * HT])\
                           .then_inc(us_cp, 1)

                with act.Fori(1, 6) as i:
                    store(i)
                with act.Fori(0, Q - 1) as q:
                    store(5 * q + 6)
                    store(5 * q + 7)
                    token_rows(q)
                    split(q)
                    for r in range(3):
                        store(5 * q + 8 + r)
                token_rows(Q - 1)
                split(Q - 1)

                act.wait_ge(km_all, 1)
                act.mul(kmx[0:KCH, 2:3], kmx[0:KCH, 1:2], -1.0).then_inc(stab, 1)
                act.wait_ge(stab, 1)

                def front(b, s, t, first=False, turn=None):
                    n = 2 * b + t
                    act.wait_ge(qk_ready, n + 1)
                    if not (first):
                        act.wait_ge(ss_done, n - 1)
                    act.activation(sq[:, t, :], p_qk[0:HT, 0:2 * D], ACT.Square).then_inc(sq_done, 1)
                    act.wait_ge(kd_ready, n + 1)
                    act.activation(ek[:, s, t, :].rearrange("p (g n) -> p g n", g=2), p_kd[0:HT, :, 0:HALF],
                                   ACT.Exp, bias=kmx[0:HT, 2:3]).then_inc(ek_done, 1)
                    if turn is not None:
                        turned(*turn)
                    act.wait_ge(ss_done, n + 1)
                    act.activation(dk[:, s, t, :], ss[:, s, t, NH:2 * NH], ACT.Exp, scale=-0.125)\
                       .then_inc(dk_done, 1)

                def tokens(b, s):
                    act.copy(u1s[:, s, :, :, 0:C], ut[:, bass.ds(2 * b, 2), :].unsqueeze(2)
                             .to_broadcast([HT, 2, 2, C])).then_inc(u1_done, 1)

                def query_exp(b, s, r):
                    act.wait_ge(qt_ps, 3 * b + r + 1)
                    act.activation(eqt[0:PM, s, 2 * r:2 * r + 2, :],
                                   p_qt[0:PM, r % 2, 0:2 * TOK].rearrange("p (a t) -> p a t", a=2),
                                   ACT.Exp).then_inc(eq_done, 1)

                def query_eps(b, s, r):
                    act.wait_ge(eq_done, 3 * b + r + 1)
                    act.activation(eqt[0:PM, s, 2 * r:2 * r + 2, :], eqt[0:PM, s, 2 * r:2 * r + 2, :], ACT.Identity,
                                   bias=epsc[0:PM, 0:1]).then_inc(eqe_done, 1)

                def turned(b, s):
                    if not (isinstance(b, int) and b < 2):
                        act.wait_ge(g_ps, b - 1)
                    act.copy(ats[0:VH, s, :, :], p_kd[0:VH, :, HALF:HALF + TOK]).then_inc(ats_done, 1)

                def rows(b):
                    act.wait_ge(g_ps, b + 1)
                    act.copy(h2v[:, bass.ds(2 * b, 2), :], p_m[0:HT, 0:2 * GC].rearrange("p (t n) -> p t n", t=2))\
                       .then_inc(h2_done, 1)

                act.wait_ge(eqt_set, 1)
                tokens(0, 0)
                front(0, 0, 0, first=True)
                front(0, 0, 1, first=True)

                def image(b, s, first=False, more=True):
                    if more:
                        if not (isinstance(b, int) and b == 0):
                            act.wait_ge(kut_ps, b)
                        tokens(b + 1, 1 - s)
                        front(b + 1, 1 - s, 0)
                    if not (isinstance(b, int) and b < 2):
                        act.wait_ge(att_ps, b - 1)
                    query_exp(b, s, 0)
                    query_exp(b, s, 1)
                    if more:
                        front(b + 1, 1 - s, 1, turn=None if first else (b - 1, 1 - s))
                    else:
                        act.wait_ge(kd_ready, 2 * B + 1)
                        turned(b - 1, 1 - s)
                    query_eps(b, s, 0)
                    query_eps(b, s, 1)
                    query_exp(b, s, 2)
                    query_eps(b, s, 2)
                    if not first:
                        rows(b - 1)

                image(0, 0, first=True)
                image(1, 1)
                image(2, 0)
                image(3, 1)
                with act.Fori(2, LAG // 2) as i:
                    image(2 * i, 0)
                    image(2 * i + 1, 1)
                for q in range(Q - 1):
                    gate_roots(act, q)
                    start = (LAG + B // Q * q) // 2
                    with act.Fori(start, min(start + B // Q // 2, B // 2 - 1)) as i:
                        image(2 * i, 0)
                        image(2 * i + 1, 1)
                image(B - 2, 0)
                image(B - 1, 1, more=False)
                act.wait_ge(kd_ready, 2 * B + 2)
                turned(B - 1, 1)
                rows(B - 1)

            @block.vector
            def _(dve):
                dve.memset(bd[:, :], 0.0).then_inc(bdz, 1)
                dve.memset(us[64:128, :], 0.0).then_inc(pads, 1)
                def pool_tiles(i, first=False, then=None):
                    for s in range(XS):
                        dve.wait_ge(x_in[s], 16 * i + 16)
                        if not first:
                            dve.wait_ge(strip_out[s], 16 * i)
                        dve.tensor_reduce(strips[:, s, :],
                                          xt[:, s, :].rearrange("p (k j l) -> p j k l", k=PATCH, l=PATCH),
                                          AX.XY, ALU.add).then_inc(pooled, 1)
                        if then is not None:
                            then(s)

                pool_tiles(0, first=True)
                dve.wait_ge(w_in, 80)
                dve.reduce_sum(cwm[:, 0:1], cw13[0:C, :], axis=AX.X).then_inc(setup_d, 1)
                dve.wait_ge(setup_d, 1)
                dve.tensor_scalar(cwm[:, 1:2], cwm[:, 0:1], 1.0 / D, None, ALU.mult).then_inc(setup_d, 1)
                dve.wait_ge(setup_d, 2)
                dve.tensor_scalar(cwc[:, :], cw13[0:C, :], cwm[:, 1:2], None, ALU.subtract).then_inc(setup_d, 1)
                dve.memset(u1s[:, :, :, :, :], 0.0).then_inc(bvm, 1)
                dve.memset(w72[:, :], 0.0).then_inc(pads, 1)
                dve.memset(sht[:, :], 0.0).then_inc(pads, 1)
                dve.memset(kuw[:, :, :], 0.0).then_inc(dz, 1)
                dve.memset(wvp[:, :, :], 0.0).then_inc(dz, 1)
                dve.memset(ats[64:96, :, :, :], 0.0).then_inc(dz, 1)
                dve.memset(ats[96:128, :, :, :], 1.0).then_inc(dz, 1)
                dve.wait_ge(bvm, 1)
                dve.memset(u1s[:, :, :, :, C:UC], 1.0).then_inc(bvm, 1)
                dve.wait_ge(setup_p, 1)
                for c in range(2):
                    dve.scalar_tensor_tensor(out=wgc[:, c, :], in0=p_qt[0:NPART, 0, 0:NE], scalar=-1.0 / D,
                                             in1=wg_s[:, c, :], op0=ALU.mult, op1=ALU.add).then_inc(dz, 1)
                dve.wait_ge(setup_a, 10)
                for g in range(2):
                    dve.tensor_tensor(bv[:, g, :, :], w12t[:, 4 + g, :].unsqueeze(1).to_broadcast([NPART, 6, C]),
                                      vmask[:, :].unsqueeze(2).to_broadcast([NPART, 6, C]), ALU.mult).then_inc(bvm, 1)
                dve.wait_ge(setup_a, 14)
                dve.tensor_copy(wparts[:, 0, :], wall[:, :]).then_inc(setup_d, 1)
                dve.wait_ge(setup_d, 4)
                dve.tensor_tensor(wall[:, :], wall[:, :], wparts[:, 0, :], ALU.subtract).then_inc(setup_d, 1)
                dve.wait_ge(setup_d, 5)
                dve.tensor_copy(wparts[:, 1, :], wall[:, :]).then_inc(setup_d, 1)
                dve.wait_ge(setup_d, 6)
                dve.tensor_tensor(wparts[:, 2, :], wall[:, :], wparts[:, 1, :], ALU.subtract).then_inc(setup_d, 1)

                def normalise(q):
                    o = 13 * q
                    t = bass.ds(QT * q, QT)
                    dve.wait_ge(pt_cp, 2 * q + 2)
                    dve.tensor_tensor(gp[:, t, :], gp[:, t, :], pt[:, t, :], ALU.mult).then_inc(ln1, 1)
                    dve.wait_ge(ln1, o + 1)
                    dve.tensor_reduce(var1[:, 5, t], gp[:, t, :], AX.X, ALU.add).then_inc(ln1, 1)
                    dve.wait_ge(ln1, o + 2)
                    dve.tensor_scalar(var1[:, 0, t], var1[:, 5, t], EPS_LN, None, ALU.add).then_inc(ln1, 1)
                    dve.wait_ge(ln1a, 4 * q + 1)
                    dve.reciprocal(var1[:, 2, t], var1[:, 1, t]).then_inc(ln1, 1)
                    dve.wait_ge(ln1, o + 4)
                    dve.tensor_tensor(var1[:, 3, t], var1[:, 2, t], var1[:, 2, t], ALU.mult).then_inc(ln1, 1)
                    dve.wait_ge(ln1, o + 5)
                    dve.tensor_tensor(var1[:, 4, t], var1[:, 3, t], var1[:, 0, t], ALU.mult).then_inc(ln1, 1)
                    dve.wait_ge(ln1, o + 6)
                    dve.tensor_scalar(var1[:, 3, t], var1[:, 4, t], -0.5, 1.5, ALU.mult, ALU.add).then_inc(ln1, 1)
                    dve.wait_ge(ln1, o + 7)
                    dve.tensor_tensor(var1[:, 5, t], var1[:, 3, t], var1[:, 2, t], ALU.mult).then_inc(ln1, 1)
                    dve.wait_ge(ln1, o + 8)
                    dve.tensor_tensor(ut[:, t, :], pt[:, t, :], var1[:, 5, t].unsqueeze(2).to_broadcast([HT, QT, C]),
                                      ALU.mult).then_inc(ln1, 1)
                    dve.wait_ge(ln1, o + 9)
                    dve.tensor_copy(uu[:, t, 0:C], ut[:, t, :]).then_inc(ln1, 1)
                    dve.wait_ge(ln1, o + 10)
                    dve.tensor_tensor(gp[:, t, :], ut[:, t, :], uu[:, t, 0:C], ALU.subtract).then_inc(ln1, 1)
                    dve.wait_ge(ln1, o + 11)
                    dve.tensor_copy(uu[:, t, 3 * C:4 * C], gp[:, t, :]).then_inc(ln1, 1)
                    dve.wait_ge(ln1, o + 12)
                    dve.tensor_tensor(uu[:, t, 5 * C:6 * C], gp[:, t, :], uu[:, t, 3 * C:4 * C], ALU.subtract)\
                       .then_inc(ln1, 1)

                def key_max(q, first=0, last=QK):
                    for n in range(first, last):
                        src = (p_kd, p_qd)[n % 2]
                        dve.wait_ge(km_ps, QK * q + n + 1)
                        dve.tensor_reduce(km[:, bass.ds(QK * q + n, 1)], src[0:KCH, :, 0:HALF], AX.XY, ALU.max)\
                           .then_inc(km_cp, 1)

                with dve.Fori(1, 6) as i:
                    pool_tiles(i)
                with dve.Fori(0, Q - 1) as q:
                    pool_tiles(5 * q + 6)
                    pool_tiles(5 * q + 7)
                    normalise(q)
                    for r in range(3):
                        def some(s):
                            k = XS * r + s
                            key_max(q, QK * k // (3 * XS), QK * (k + 1) // (3 * XS))

                        pool_tiles(5 * q + 8 + r, then=some)
                normalise(Q - 1)
                key_max(Q - 1)
                dve.wait_ge(km_cp, T // KCH)
                dve.tensor_reduce(kmx[0:KCH, 0:1], km[:, :], AX.X, ALU.max).then_inc(km_fin, 1)


                dve.memset(seen[:, :], 0.0).then_inc(pads, 1)
                dve.wait_ge(pads, 4)

                def squares(b, s, t):
                    dve.wait_ge(sq_done, 2 * b + t + 1)
                    dve.tensor_reduce(ss[:, s, t, :], sq[:, t, :].rearrange("p (h d) -> p h d", d=HD), AX.X, ALU.add)\
                       .then_inc(ss_done, 1)

                def query_max(b, s, t):
                    dve.wait_ge(qd_ready, 2 * b + t + 1)
                    dve.tensor_reduce(qm[:, s, t, :].rearrange("p (g h) -> p g h", g=2),
                                      p_qd[0:HT, :, 0:HALF].rearrange("p g (h m) -> p g h m", m=M),
                                      AX.X, ALU.max).then_inc(qm_done, 1)

                def shift(b, s):
                    dve.wait_ge(ss_done, 2 * b + 2)
                    dve.wait_ge(qm_done, 2 * b + 2)
                    if not (isinstance(b, int) and b == 0):
                        dve.wait_ge(sh_ps, b)
                    dve.scalar_tensor_tensor(out=shf[:, 0], in0=ss[:, s, :, 0:NH], scalar=0.125, in1=qm[:, s],
                                             op0=ALU.mult, op1=ALU.add).then_inc(sh_step, 1)
                    dve.wait_ge(sh_step, 6 * b + 1)
                    dve.tensor_copy(s3[:, :, 0:NH], shf[:, 0]).then_inc(sh_step, 1)
                    dve.wait_ge(sh_step, 6 * b + 2)
                    dve.tensor_tensor(shf[:, 1], shf[:, 0], s3[:, :, 0:NH], ALU.subtract).then_inc(sh_step, 1)
                    dve.wait_ge(sh_step, 6 * b + 3)
                    dve.tensor_copy(s3[:, :, NH:2 * NH], shf[:, 1]).then_inc(sh_step, 1)
                    dve.wait_ge(sh_step, 6 * b + 4)
                    dve.tensor_tensor(shf[:, 2], shf[:, 1], s3[:, :, NH:2 * NH], ALU.subtract).then_inc(sh_step, 1)
                    dve.wait_ge(sh_step, 6 * b + 5)
                    dve.tensor_copy(s3[:, :, 2 * NH:3 * NH], shf[:, 2]).then_inc(sh_step, 1)

                def spread(b, s):
                    if not (isinstance(b, int) and b < 2):
                        dve.wait_ge(att_ps, b - 1)
                    dve.wait_ge(ku_ps, b + 1)
                    for g in range(2):
                        at0 = g * (3 * WIN + 2 * UC)
                        src = p_m[0:PM, 0:3 * 2 * UW].rearrange("p (a g c) -> p a g c", a=3, g=2)[:, :, g, 0:UC]
                        dve.tensor_tensor(
                            kuw[0:PM, s, at0:at0 + 3 * STEP].rearrange("p (a w) -> p a w", a=3)[:, :, 0:2 * UC]
                            .rearrange("p a (e c) -> p a e c", e=2),
                            src.unsqueeze(2).to_broadcast([PM, 3, 2, UC]), umask[:, :, :, :], ALU.mult)\
                           .then_inc(kuw_done, 1)

                def statistics(b):
                    dve.wait_ge(h2_done, b + 1)
                    for t in range(2):
                        dve.bn_stats(bn[:, bass.ds(2 * b + t, 1), :].rearrange("p a n -> p (a n)"),
                                     h2v[:, bass.ds(2 * b + t, 1), 0:D].rearrange("p a n -> p (a n)"))\
                           .then_inc(bn_done, 1)

                def shifted(b):
                    dve.wait_ge(sh_ps, b + 1)
                    dve.tensor_copy(sht[0:3 * NH, :], p_qd[0:3 * NH, 0, HALF:HALF + TOK]).then_inc(sht_done, 1)

                for t in range(2):
                    squares(0, 0, t)
                    query_max(0, 0, t)
                shift(0, 0)
                shifted(0)

                def send(b, s, t, part):
                    if part is not None:
                        n = 2 * (b - LAG) + t
                        if not (isinstance(b, int) and b < LAG + 2):
                            dve.wait_ge(hb_out[2 * s + t], 16 * (b - s - LAG))
                        token_rows(dve, n, n - QT * part, 2 * s + t)

                def image(b, s, first=False, more=True, part=None):
                    if more:
                        squares(b + 1, 1 - s, 0)
                        query_max(b + 1, 1 - s, 0)
                    send(b, s, 0, part)
                    dve.wait_ge(kut_ps, b + 1)
                    dve.tensor_scalar(kut[:, :], p_m[0:2 * UW, 0:HALF], p_m[0:2 * UW, HALF:HALF + 1], None, ALU.add)\
                       .then_inc(kut_done, 1)
                    if more:
                        squares(b + 1, 1 - s, 1)
                    spread(b, s)
                    if more:
                        query_max(b + 1, 1 - s, 1)
                        shift(b + 1, 1 - s)
                        shifted(b + 1)
                    if not first:
                        statistics(b - 1)
                    send(b, s, 1, part)
                    dve.wait_ge(att_ps, b + 1)
                    a = p_qt[0:HT, 1, 0:2 * NH * UC].rearrange("p (t h c) -> p t h c", t=2, c=UC)
                    dve.reciprocal(rd[:, :, :], a[:, :, :, C]).then_inc(rd_done, 1)
                    dve.wait_ge(rd_done, b + 1)
                    for t in range(2):
                        dve.tensor_tensor(at[:, s, t, :].rearrange("p (h d) -> p h d", d=C), a[:, t, :, 0:C],
                                          rd[:, t, :].unsqueeze(2).to_broadcast([HT, NH, C]), ALU.mult)\
                           .then_inc(at_done, 1)

                image(0, 0, first=True)
                image(1, 1)
                image(2, 0)
                image(3, 1)
                with dve.Fori(2, LAG // 2) as i:
                    image(2 * i, 0)
                    image(2 * i + 1, 1)
                for q in range(Q - 1):
                    gate(dve, q)
                    if q == 0:
                        image(LAG, 0, part=0)
                        image(LAG + 1, 1, part=0)
                    start = (LAG + B // Q * q) // 2
                    with dve.Fori(start + (q == 0), min(start + B // Q // 2, B // 2 - 1)) as i:
                        image(2 * i, 0, part=q)
                        image(2 * i + 1, 1, part=q)
                image(B - 2, 0, part=Q - 2)
                image(B - 1, 1, more=False, part=Q - 2)
                statistics(B - 1)
                for n in range(2 * (B - LAG), QT * (Q - 1)):
                    dve.wait_ge(hb_out[n % XSL], 32 * (n // XSL))
                    token_rows(dve, n, n - QT * (Q - 2), n % XSL)

            @block.tensor
            def _(pe):
                pe.wait_ge(cst, 19)
                pe.wait_ge(setup_d, 3)
                for c in range(2):
                    cols = slice(NPART * c, NPART * c + NPART)
                    pe.transpose(p_m[0:NPART, C * c:C * c + C], cwc[:, cols], ident[0:C, 0:C])
                    pe.transpose(p_m[0:NPART, 32 + (C + 1) * c:32 + (C + 1) * (c + 1)], cw13[:, cols],
                                 ident[0:C + 1, 0:C + 1])
                    for g in range(2):
                        pe.transpose(p_m[0:NPART, 64 + D * c + NPART * g:64 + D * c + NPART * (g + 1)],
                                     wproj_s[:, g, cols], ident[0:NPART, 0:NPART])
                for c in range(2):
                    mm = pe.matmul(p_qt[0:NPART, 0, 0:NE], ones[0:NPART, 0:NPART], wg_s[:, c, :],
                                   start=(c == 0), stop=(c == 1))
                mm.then_inc(setup_p, 1)
                pe.wait_ge(setup_a, 3)
                pe.wait_ge(dz, 6)
                for c in range(2):
                    pe.matmul(p_kd[0:C, 0, 0:2 * D], cwct[:, c, :], wqkv_s[:, c, 0:2 * D], start=(c == 0), stop=(c == 1))
                for g in range(6):
                    for c in range(2):
                        pe.matmul(p_qd[0:NPART, 0, C * g:C * g + C], wqkv_s[:, c, NPART * g:NPART * g + NPART],
                                  cwct[:, c, :], start=(c == 0), stop=(c == 1))
                for c in range(2):
                    pe.matmul(p_qd[0:C, 1, 0:C], cwct[:, c, :], cwct[:, c, :], start=(c == 0), stop=(c == 1))
                for c in range(2):
                    pe.matmul(p_qk[0:C + 1, 0:NE], cw13t[:, c, :], wgc[:, c, :], start=(c == 0), stop=(c == 1))
                for g in range(2):
                    for c in range(2):
                        mm = pe.matmul(p_qk[0:NPART, 16 + 16 * g:16 + 16 * g + NE], wpt[:, c, NPART * g:NPART * g + NPART],
                                       wgc[:, c, :], start=(c == 0), stop=(c == 1))
                mm.then_inc(setup_p, 1)
                pe.wait_ge(setup_a, 10)
                pe.wait_ge(bd_in, 96)
                pe.wait_ge(bvm, 4)
                for g in range(2):
                    pe.matmul(p_m[0:VH, GC * g:GC * g + GC], bv[:, g, :, :].rearrange("p h c -> p (h c)"),
                              wproj_s[:, g, :], start=True, stop=True)
                for g in range(4):
                    dst = (p_kd, p_kd, p_qt, p_qt)[g]
                    mm = pe.matmul(dst[0:C, g % 2, 0:HALF], w12t[:, g, :], bd[:, :], start=True, stop=True)
                mm.then_inc(setup_p, 1)

                pe.wait_ge(setup_a, 16)
                pe.wait_ge(w72_in, 96)

                def part(q):
                    if isinstance(q, int):
                        pe.wait_ge(pc_last, 16)
                    else:
                        pe.wait_ge(pc_in, 16 * q + 16)
                    for t in range(QT):
                        pe.matmul(p_qk[0:HT, C * t:C * t + C], pcr[:, HT * t:HT * t + HT], gram[:, :],
                                  start=True, stop=True)
                    for t in range(QT):
                        mm = pe.transpose(p_m[0:HT, C * t:C * t + C], pcr[:, HT * t:HT * t + HT], ident[0:C, 0:C])
                    mm.then_inc(pt_ps, 1)
                    pe.wait_ge(ln1, 13 * q + 13)
                    pe.wait_ge(ln1a, 4 * q + 4)
                    for g in range(QT // GG):
                        if g > 1:
                            pe.wait_ge(us_cp, QT // GG * q + g - 1)
                        for t in range(GG):
                            mm = pe.matmul(p_kd[0:K6, g % 2, HT * t:HT * t + HT],
                                           uu[:, bass.ds(QT * q + GG * g + t, 1), :].rearrange("p a n -> p (a n)"),
                                           identb[0:HT, 0:HT], start=True, stop=True)
                        mm.then_inc(us_ps, 1)
                    pe.wait_ge(us_cp, QT // GG * (q + 1))
                    for n in range(QK):
                        dst = (p_kd, p_qd)[n % 2]
                        if n > 1:
                            pe.wait_ge(km_cp, QK * q + n - 1)
                        for g in range(2):
                            mm = pe.matmul(dst[0:KCH, g, 0:HALF], us[:, bass.ds(KCH * (QK * q + n), KCH)],
                                           w72[:, CDK + HALF * g:CDK + HALF * g + HALF], start=True, stop=True)
                        mm.then_inc(km_ps, 1)

                with pe.Fori(0, Q - 1) as q:
                    part(q)
                part(Q - 1)
                pe.wait_ge(km_cp, T // KCH)

                def front(b, t, turned=None):
                    n = 2 * b + t
                    u = us[:, bass.ds(TOK * b + HT * t, HT)]
                    fresh = isinstance(b, int) and b == 0 and t == 0
                    if not fresh:
                        pe.wait_ge(sq_done, n)
                    pe.matmul(p_qk[0:HT, 0:2 * D], u, w72[:, 0:2 * D], start=True, stop=True).then_inc(qk_ready, 1)
                    if not fresh:
                        pe.wait_ge(ek_done, n)
                    if t == 0 and not (isinstance(b, int) and b < 3):
                        pe.wait_ge(ats_done, b - 2)
                    for g in range(2):
                        mm = pe.matmul(p_kd[0:HT, g, 0:HALF], u, w72[:, CDK + HALF * g:CDK + HALF * g + HALF],
                                  start=True, stop=True)
                    if turned is not None:
                        mm = turn_rows(*turned)
                    mm.then_inc(kd_ready, 1)
                    if not fresh:
                        pe.wait_ge(qm_done, n)
                        if t == 0:
                            pe.wait_ge(sht_done, b)
                    for g in range(2):
                        mm = pe.matmul(p_qd[0:HT, g, 0:HALF], u, w72[:, CDQ + HALF * g:CDQ + HALF * g + HALF],
                                       start=True, stop=True)
                    mm.then_inc(qd_ready, 1)

                def turn_rows(b, s):
                    pe.wait_ge(at_done, 2 * b + 2)
                    for t in range(2):
                        for g in range(2):
                            mm = pe.transpose(p_kd[0:VH, g, HALF + HT * t:HALF + HT * t + HT],
                                              at[:, s, t, VH * g:VH * g + VH], ident[0:HT, 0:HT])
                    return mm

                def queries(b, s, r):
                    u = us[:, bass.ds(TOK * b, TOK)]
                    for a in range(2):
                        p = 2 * r + a
                        pe.matmul(p_qt[0:PM, r % 2, TOK * a:TOK * a + TOK], w72[:, CDQ + PM * p:CDQ + PM * p + PM], u,
                                  start=True, stop=False)
                        mm = pe.matmul(p_qt[0:PM, r % 2, TOK * a:TOK * a + TOK], ind3[:, PM * p:PM * p + PM], sht[:, :],
                                       start=False, stop=True)
                    mm.then_inc(qt_ps, 1)

                def channel_keys(b, s):
                    pe.wait_ge(k1_done, 2 * b + 2)
                    pe.wait_ge(u1_done, b + 1)
                    for g in range(2):
                        for t in range(2):
                            pe.matmul(p_m[UW * g:UW * g + UW, 0:HALF], u1s[:, s, t, g, :],
                                      ek[:, s, t, HALF * g:HALF * g + HALF], start=(t == 0), stop=(t == 1))
                    for t in range(2):
                        mm = pe.matmul(p_m[0:2 * UW, HALF:HALF + 1], u1s[:, s, t, :, :].rearrange("p g c -> p (g c)"),
                                       epsc[0:HT, 0:1], start=(t == 0), stop=(t == 1))
                    mm.then_inc(kut_ps, 1)

                def key_channels(b):
                    pe.wait_ge(cst, 19)
                    pe.wait_ge(kut_done, b + 1)
                    for a in range(3):
                        mm = pe.transpose(p_m[0:PM, 2 * UW * a:2 * UW * (a + 1)], kut[:, PM * a:PM * a + PM],
                                          ident[0:2 * UW, 0:2 * UW])
                    mm.then_inc(ku_ps, 1)

                def attend(b, s):
                    pe.wait_ge(kuw_done, 2 * b + 2)
                    pe.wait_ge(eqe_done, 3 * b + 3)
                    for t in range(2):
                        for p in range(PAIRS):
                            col = NH * UC * t + (0 if p < 3 else 4 * UC)
                            mm = pe.matmul(p_qt[0:HT, 1, col:col + WIN], eqt[:, s, p, HT * t:HT * t + HT],
                                           kuw[:, s, WIN * p:WIN * p + WIN], start=(p == 0), stop=(p == PAIRS - 1),
                                           skip_group_check=True)
                    mm.then_inc(att_ps, 1)

                def project(b, s):
                    pe.wait_ge(ats_done, b + 1)
                    pe.wait_ge(pl_in[s], 8 * (b - s) + 16)
                    for t in range(2):
                        pe.matmul(p_m[0:HT, GC * t:GC * t + GC], ats[:, s, 0, HT * t:HT * t + HT], wvp[:, 0, :],
                                  start=True, stop=False)
                        mm = pe.matmul(p_m[0:HT, GC * t:GC * t + GC], ats[:, s, 1, HT * t:HT * t + HT],
                                       wvp[:, 1, :], start=False, stop=True)
                    mm.then_inc(g_ps, 1)

                def turn_shift(b):
                    pe.wait_ge(sh_step, 6 * b + 6)
                    for t in range(2):
                        mm = pe.matmul(p_qd[0:3 * NH, 0, HALF + HT * t:HALF + HT * t + HT], s3[:, t, :],
                                       negib[0:HT, 0:HT], start=True, stop=True)
                    mm.then_inc(sh_ps, 1)

                pe.wait_ge(cwg_in, 16)
                front(0, 0)
                front(0, 1)
                turn_shift(0)

                def image(b, s, first=False, more=True):
                    if more:
                        front(b + 1, 0)
                    pe.wait_ge(sht_done, b + 1)
                    if not first:
                        pe.wait_ge(eq_done, 3 * b)
                    queries(b, s, 0)
                    if not first and not (isinstance(b, int) and b < 2):
                        pe.wait_ge(h2_done, b - 1)
                    channel_keys(b, s)
                    if not first:
                        pe.wait_ge(at_done, 2 * b)
                    queries(b, s, 1)
                    if more:
                        front(b + 1, 1, None if first else (b - 1, 1 - s))
                    else:
                        pe.wait_ge(ek_done, 2 * B)
                        pe.wait_ge(ats_done, b - 1)
                        turn_rows(b - 1, 1 - s).then_inc(kd_ready, 1)
                    key_channels(b)
                    pe.wait_ge(eq_done, 3 * b + 1)
                    queries(b, s, 2)
                    if not first:
                        pe.wait_ge(kuw_done, 2 * b + 2)
                        project(b - 1, 1 - s)
                    if more:
                        turn_shift(b + 1)
                    attend(b, s)

                image(0, 0, first=True)
                image(1, 1)
                image(2, 0)
                image(3, 1)
                with pe.Fori(2, LAG // 2) as i:
                    image(2 * i, 0)
                    image(2 * i + 1, 1)
                for q in range(Q - 1):
                    pe.wait_ge(h2_done, LAG + B // Q * q - 1)
                    gate_counts(pe, q)
                    start = (LAG + B // Q * q) // 2
                    with pe.Fori(start, min(start + B // Q // 2, B // 2 - 1)) as i:
                        image(2 * i, 0)
                        image(2 * i + 1, 1)
                image(B - 2, 0)
                image(B - 1, 1, more=False)
                pe.wait_ge(ats_done, B - 1)
                turn_rows(B - 1, 1).then_inc(kd_ready, 1)
                pe.wait_ge(h2_done, B - 1)
                project(B - 1, 1)

        with nc.Block() as block:

            @block.gpsimd
            def _(pool):
                pool.memset(pad[:, :, :, :], 0.0).then_inc(tables, 1)
                pool.wait_ge(tables, 7)

                def set_pad(n, s):
                    pool.tensor_copy(pad[:, s, :, D:D + 1], padi[:, bass.ds(n, 1), :].rearrange("p a q -> p q a"))\
                        .then_inc(pad_set, 1)

                for s in range(PSL):
                    set_pad(s, s)
                with pool.Fori(1, (NE + SPARE) // PSL) as i:
                    for s in range(PSL):
                        pool.wait_ge(pad_out[s], 16 * i)
                        set_pad(PSL * i + s, s)

                with pool.Fori(NT // XSL // Q * (Q - 1), NT // XSL) as i:
                    for s in range(XSL):
                        scatter(pool, XSL * i + s, s)
                for s in range(XSL):
                    pool.wait_ge(hb_out[s], 32 * (NT // XSL))

            @block.sync
            def _(sp):
                def send_pad(n, row):
                    sp.wait_ge(pad_set, n + 1)
                    sp.dma_start(slots_d[bass.ds(row, ST), :].rearrange("(p q) n -> p q n", q=SQ),
                                 pad[:, n % PSL, :, :]).then_inc(pad_out[n % PSL], 16)

                for n in range(SPARE):
                    send_pad(n, NE * REG + n * ST)
                sp.wait_ge(gate_d, GSTEPS * Q + 12)
                for n in range(NE):
                    send_pad(SPARE + n, sp.value_load(where[0:1, 2 * ETILES + n:2 * ETILES + n + 1],
                                                      min_val=0, max_val=NE * REG - ST))
                for s in range(PSL):
                    sp.wait_ge(pad_out[s], 16 * (NE + SPARE) // PSL)

            @block.scalar
            def _(act):
                gate_roots(act, Q - 1)

            @block.tensor
            def _(pe):
                gate_counts(pe, Q - 1)

            @block.vector
            def _(dve):
                gate(dve, Q - 1)

                def steps(n):
                    dve.wait_ge(gate_d, GSTEPS * Q + n)

                def tt(out, a, b, op):
                    dve.tensor_tensor(out, a, b, op).then_inc(gate_d, 1)

                steps(0)
                cnt = seen[:, :]
                c = cx[0:HT]
                big = float(1 << 23)
                dve.tensor_scalar(c[:, 0, :], cnt, 1.0 / ST, (ST - 1) / (2.0 * ST), ALU.mult, ALU.add).then_inc(gate_d, 1)
                steps(1)
                dve.tensor_scalar(c[:, 1, :], c[:, 0, :], big, None, ALU.add).then_inc(gate_d, 1)
                steps(2)
                dve.tensor_scalar(c[:, 2, :], c[:, 1, :], big, None, ALU.subtract).then_inc(gate_d, 1)
                steps(3)
                dve.tensor_tensor_scan(c[:, 3, :], c[:, 2, :], ones[0:HT, 0:NE], 0.0, ALU.add, ALU.mult).then_inc(gate_d, 1)
                dve.tensor_scalar(c[:, 4, :], c[:, 2, :], -float(ST), float(REG), ALU.mult, ALU.add).then_inc(gate_d, 1)
                steps(5)
                done = tl[0:HT, 0]
                number = tabf[0:HT, 2 * NE:2 * NE + ETILES]
                tt(done, c[:, 3, :].unsqueeze(1).to_broadcast([HT, ETILES, NE]),
                   number.unsqueeze(2).to_broadcast([HT, ETILES, NE]), ALU.is_le)
                steps(6)
                tt(tl[0:HT, 1], done, c[:, 4, :].unsqueeze(1).to_broadcast([HT, ETILES, NE]), ALU.mult)
                dve.tensor_reduce(tj[0:HT, 0], done, AX.X, ALU.add).then_inc(gate_d, 1)
                steps(8)
                dve.tensor_reduce(tj[0:HT, 1], tl[0:HT, 1], AX.X, ALU.add).then_inc(gate_d, 1)
                dve.tensor_scalar(where[:, ETILES:2 * ETILES], tj[0:1, 0], NE - 1.0, None, ALU.min).then_inc(gate_d, 1)
                steps(10)
                dve.scalar_tensor_tensor(out=where[:, 0:ETILES], in0=number[0:1], scalar=float(ST), in1=tj[0:1, 1],
                                         op0=ALU.mult, op1=ALU.add).then_inc(gate_d, 1)
                tt(where[:, 2 * ETILES:], cnt[0:1], tabf[0:1, NE:2 * NE], ALU.add)
                steps(12)


                with dve.Fori(NT // XSL // Q * (Q - 1), NT // XSL) as i:
                    for s in range(XSL):
                        dve.wait_ge(hb_out[s], 32 * i)
                        token_rows(dve, XSL * i + s, XSL * i + s - QT * (Q - 1), s)

        with nc.Block() as block:

            @block.sync
            def _(sp):
                def place(n):
                    return (sp.value_load(where[0:1, bass.ds(n, 1)], min_val=0, max_val=XROWS - ST),
                            sp.value_load(where[0:1, bass.ds(n + ETILES, 1)], min_val=0, max_val=NE - 1))

                def load_x(row, s):
                    sp.dma_start(xin[:, s, :, :], slots_d[bass.ds(row, ST), :].rearrange("(p q) n -> p q n", q=SQ))\
                      .then_inc(x_ld[s], 16)

                def load_w1(e, s):
                    sp.dma_start(w1t[:, s, :].rearrange("p (c n) -> p c n", c=2),
                                 w1[bass.ds(e, 1)].rearrange("a (c p) n -> (a p) c n", p=NPART))\
                      .then_inc(w1_ld[s], 16)

                def load_w2(e, s):
                    sp.dma_start(b1t[:, s, :], b1[bass.ds(e, 1)].rearrange("a (m p) -> (a p) m", p=128),
                                 allow_slow_non_contiguous=True).then_inc(w2_ld[s], 16)
                    sp.dma_start(w2t[:, s, :, :], w2[bass.ds(e, 1)].rearrange("a (m p) n -> (a p) m n", p=128))\
                      .then_inc(w2_ld[s], 16)
                    sp.dma_start(b2t[:, s, :], b2[bass.ds(e, 1)].to_broadcast([128, D]))\
                      .then_inc(w2_ld[s], 16)

                for s in range(2):
                    row, e = place(s)
                    load_x(row, s)
                    load_w1(e, s)
                    load_w2(e, s)
                with sp.Fori(1, ETILES // 2) as i:
                    for s in range(2):
                        row, e = place(2 * i + s)
                        sp.wait_ge(ypr_done, 2 * i + s - 1)
                        sp.sem_inc(begun, 1)
                        load_x(row, s)
                        sp.wait_ge(w1_lo, 2 * i + s - 1)
                        sp.sem_inc(begun, 1)
                        load_w1(e, s)
                        sp.wait_ge(ys_b, 2 * i + s - 1)
                        sp.sem_inc(begun, 1)
                        load_w2(e, s)

            @block.tensor
            def _(pe):
                def turn(n, i, s, first=False):
                    pe.wait_ge(x_ld[s], 16 * i + 16)
                    if not first:
                        pe.wait_ge(xt_done, 2 * n)
                    for c in range(2):
                        for q in range(SQ):
                            mm = pe.transpose(p_kd[0:NPART, c, 128 * q:128 * q + 128],
                                              xin[:, s, q, NPART * c:NPART * c + NPART], ident[:, :])
                    mm.then_inc(xt_ps, 1)

                PARTS = ((0, 0), (0, 1), (1, 0))

                def hidden(n, first=False):
                    pe.wait_ge(w1_lo, n + 1)
                    pe.wait_ge(xt_done, 2 * n + 2)
                    for m in range(3):
                        if not first:
                            pe.wait_ge(hid_done, 3 * n + m - 2)
                        for k in range(6):
                            c, (a, b) = k // 3, PARTS[k % 3]
                            mm = pe.matmul((p_qk, p_m, p_qd[:, 0, :])[m][:, :],
                                           w1r[:, a, HID * c + 128 * m:HID * c + 128 * m + 128],
                                           xtr[:, b, c, :], start=(k == 0), stop=(k == 5))
                        mm.then_inc(hid_ps, 1)

                def output(n, i, s, first=False):
                    pe.wait_ge(w2_ld[s], 48 * i + 48)
                    pe.wait_ge(hid_done, 3 * n + 3)
                    if not first:
                        pe.wait_ge(ys_b, n)
                    for q in range(SQ):
                        for m in range(3):
                            mm = pe.matmul(p_qt[:, q // 2, D * (q % 2):D * (q % 2) + D],
                                           hid[:, m, 128 * q:128 * q + 128], w2t[:, s, m, :],
                                           start=(m == 0), stop=(m == 2))
                    mm.then_inc(ys_ps, 1)

                turn(0, 0, 0, first=True)
                hidden(0, first=True)
                turn(1, 0, 1)
                output(0, 0, 0, first=True)
                with pe.Fori(0, ETILES // 2 - 1) as i:
                    for s in range(2):
                        n = 2 * i + s + 1
                        hidden(n)
                        turn(n + 1, i + 1, s)
                        output(n, i + s, 1 - s)
                hidden(ETILES - 1)
                output(ETILES - 1, ETILES // 2 - 1, 1)

            @block.scalar
            def _(act):
                def tile(n, i, s):
                    act.wait_ge(w2_ld[s], 48 * i + 48)
                    for m in range(3):
                        act.wait_ge(hid_ps, 3 * n + m + 1)
                        act.activation(hid[:, m, :], (p_qk, p_m, p_qd[:, 0, :])[m][:, :], ACT.Gelu,
                                       bias=b1t[:, s, m:m + 1]).then_inc(hid_done, 1)

                def highs(n, first=False):
                    act.wait_ge(xt_ps, n + 1)
                    if not first:
                        act.wait_ge(hid_ps, 3 * n)
                    for c in range(2):
                        act.copy(xtr[:, 0, c, :], p_kd[0:NPART, c, :]).then_inc(xt_hi, 1)

                def weight_high(n, i, s, first=False):
                    act.wait_ge(w1_ld[s], 16 * i + 16)
                    if not first:
                        act.wait_ge(hid_ps, 3 * n)
                    act.copy(w1r[:, 0, :], w1t[:, s, :]).then_inc(w1_hi, 1)

                weight_high(0, 0, 0, first=True)
                highs(0, first=True)
                tile(0, 0, 0)
                highs(1)
                weight_high(1, 0, 1)
                with act.Fori(0, ETILES // 2 - 1) as i:
                    for s in range(2):
                        n = 2 * i + s + 2
                        tile(n - 1, i + s, 1 - s)
                        highs(n)
                        weight_high(n, i + 1, s)
                tile(ETILES - 1, ETILES // 2 - 1, 1)

            @block.vector
            def _(dve):
                def turned(n, s, first=False):
                    dve.wait_ge(xt_ps, n + 1)
                    for c in range(2):
                        dve.wait_ge(xt_hi, 2 * n + c + 1)
                        dve.tensor_tensor(xtr[:, 1, c, :], p_kd[0:NPART, c, :], xtr[:, 0, c, :].bitcast(F32),
                                          ALU.subtract).then_inc(xt_done, 1)
                    if not first:
                        dve.wait_ge(ys_done, n - 1)
                    dve.tensor_copy(ypr[:, s, :, :], xin[:, s, :, D:ROW]).then_inc(ypr_done, 1)

                def weight_low(n, s):
                    dve.wait_ge(w1_hi, n + 1)
                    dve.tensor_tensor(w1r[:, 1, :], w1t[:, s, :], w1r[:, 0, :].bitcast(F32), ALU.subtract)\
                       .then_inc(w1_lo, 1)

                def results(n, i, s, first=False):
                    dve.wait_ge(ys_ps, n + 1)
                    if not first:
                        dve.wait_ge(ys_out[s], 64 * i)
                    dve.wait_ge(ypr_done, n + 1)
                    dve.tensor_copy(ydst[:, s, :], ypr[:, s, :, 0]).then_inc(ydst_done, 1)
                    y = ys[:, s, :, :]
                    dve.tensor_tensor(y.rearrange("p (g q) n -> p g q n", g=2),
                                      p_qt[:, :, 0:2 * D].rearrange("p g (q n) -> p g q n", q=2),
                                      b2t[:, s, :].unsqueeze(1).unsqueeze(1).to_broadcast([128, 2, 2, D]), ALU.add)\
                       .then_inc(ys_b, 1)

                weight_low(0, 0)
                turned(0, 0, first=True)
                turned(1, 1, first=True)
                weight_low(1, 1)
                results(0, 0, 0, first=True)
                turned(2, 0)
                weight_low(2, 0)
                results(1, 0, 1, first=True)
                with dve.Fori(1, ETILES // 2 - 1) as i:
                    for s in range(2):
                        turned(2 * i + s + 1, 1 - s)
                        weight_low(2 * i + s + 1, 1 - s)
                        results(2 * i + s, i, s)
                turned(ETILES - 1, 1)
                weight_low(ETILES - 1, 1)
                results(ETILES - 2, ETILES // 2 - 1, 0)
                results(ETILES - 1, ETILES // 2 - 1, 1)

            @block.gpsimd
            def _(pool):
                with pool.Fori(0, ETILES // 2) as i:
                    for s in range(2):
                        n = 2 * i + s
                        pool.wait_ge(ys_b, n + 1)
                        pool.wait_ge(ydst_done, n + 1)
                        pool.tensor_tensor(ys[:, s, :, :], ys[:, s, :, :],
                                           ypr[:, s, :, 1:2].to_broadcast([128, SQ, D]), ALU.mult)\
                            .then_inc(ys_done, 1)
                        pool.wait_ge(ys_done, n + 1)
                        pool.sem_inc(sent, 1)
                        for q in range(SQ):
                            pool.indirect_dma_start(
                                out=y_d[:, :], out_offset=bass.IndirectOffsetOnAxis(ap=ydst[:, s, q:q + 1], axis=0),
                                in_=ys[:, s, q, :], in_offset=None).then_inc(ys_out[s], 16)
                for s in range(2):
                    pool.wait_ge(ys_out[s], 64 * (ETILES // 2))

        y_v = y_d[0:2 * T, :].rearrange("(k t p) n -> t k p n", k=2, p=HT)
        out_v = out.rearrange("b (h p) n -> (b h) p n", p=HT)
        with nc.Block() as block:

            @block.sync
            def _(sp):
                def load(g, s):
                    for t in range(GG):
                        sp.dma_start(yin[:, s, t, :, :],
                                     y_v[bass.ds(GG * g + t, 1)].rearrange("a k p n -> (a p) k n"))\
                          .then_inc(yin_ld[s], 16)

                for s in range(YSL):
                    load(s, s)
                with sp.Fori(1, NT // GG // YSL) as i:
                    for s in range(YSL):
                        sp.wait_ge(sum1, YSL * i + s - YSL + 1)
                        load(YSL * i + s, s)

            @block.vector
            def _(dve):
                with dve.Fori(0, NT // GG // YSL) as i:
                    for s in range(YSL):
                        g = YSL * i + s
                        dve.wait_ge(yin_ld[s], 16 * GG * (i + 1))
                        rows = h2v[:, bass.ds(GG * g, GG), 0:D]
                        dve.tensor_tensor(yin[:, s, :, 0, :], yin[:, s, :, 0, :], yin[:, s, :, 1, :], ALU.add)\
                           .then_inc(sum0, 1)
                        dve.wait_ge(sum0, g + 1)
                        dve.tensor_tensor(rows, rows, yin[:, s, :, 0, :], ALU.add).then_inc(sum1, 1)

            @block.scalar
            def _(act):
                with act.Fori(0, NT // GG) as g:
                    act.wait_ge(sum1, g + 1)
                    act.dma_start(out_v[bass.ds(GG * g, GG)].rearrange("t p n -> p t n"),
                                  h2v[:, bass.ds(GG * g, GG), 0:D]).then_inc(o_out, 16)
                act.wait_ge(o_out, 16 * (NT // GG))


_INS = ['x', 'L0_tok_channel_weights', 'L0_attn_W_qkv', 'L0_attn_W_proj', 'L0_attn_b_proj', 'L0_attn_proj_mat',
        'L0_ffn_Wg', 'L0_ffn_W1', 'L0_ffn_b1', 'L0_ffn_W2', 'L0_ffn_b2']
_OUTS = [((64, 196, 192), 'float32')]


def kernel(**inputs):
    import numpy as _np
    import concourse.bacc as _bacc
    from concourse import mybir as _mybir
    from concourse.bass_utils import run_bass_kernel_spmd as _run

    nc = _bacc.Bacc("TRN2", target_bir_lowering=False, num_devices=1)
    arrays, args = {}, []
    for name in _INS:
        a = _np.ascontiguousarray(inputs[name])
        arrays[f"in_{name}_dram"] = a
        args.append(nc.dram_tensor(f"in_{name}_dram", a.shape, _mybir.dt.from_np(a.dtype), kind="ExternalInput").ap())
    for i, (shape, dtype) in enumerate(_OUTS):
        dt = _mybir.dt.from_np(_np.dtype(dtype))
        args.append(nc.dram_tensor(f"out_{i}_dram", shape, dt, kind="ExternalOutput").ap())
    vit_block(nc, *args)
    r = _run(nc, [arrays], core_ids=[0])
    got = tuple(r.results[0][f"out_{i}_dram"] for i in range(len(_OUTS)))
    return got[0]
```
